# Optimizing a Trainium2 kernel written in Bass

```python
import numpy as np
import jax
import jax.numpy as jnp

def _softmax(x, axis=-1):
    return jax.nn.softmax(x, axis=axis)

def _gelu(x):
    return jax.nn.gelu(x, approximate=True)

def _silu(x):
    return jax.nn.silu(x)

def _sigmoid(x):
    return jax.nn.sigmoid(x)

def _layernorm(x, axis=-1, eps=1e-05):
    m = jnp.mean(x, axis=axis, keepdims=True)
    v = jnp.var(x, axis=axis, keepdims=True)
    return (x - m) / jnp.sqrt(v + eps)

def _scatter_add(tgt, idx, src, axis=0):
    return tgt.at[idx].add(src)

def _segment_sum(src, seg, n):
    return jax.ops.segment_sum(src, seg, n)
kernel_name = 'mk_gps_d1_gnn_r8_a77719'

def setup_inputs(seed: int=0):
    np.random.seed(seed)
    _w = jnp.asarray

    def _rec_inputs():
        import jax
        import jax.numpy as jnp
        _gk = jax.random.key(seed)
        x = -0.0003713 + 1 * jax.random.normal(jax.random.fold_in(_gk, 1), (6250, 256), jnp.float32)
        _s = jax.random.randint(jax.random.fold_in(_gk, 2), (100000,), 0, 6250, jnp.int32)
        _d = jax.random.randint(jax.random.fold_in(_gk, 3), (100000,), 0, 6250, jnp.int32)
        _loop = jnp.arange(6250, dtype=jnp.int32)
        src = jnp.concatenate([_s, _d, _loop])
        dst = jnp.concatenate([_d, _s, _loop])
        _o = jnp.argsort(dst, stable=True)
        src = src[_o]
        dst = dst[_o]
        edge_attr_3 = -1.09012e-05 + 0.99985 * jax.random.normal(jax.random.fold_in(_gk, 11), (206250, 3), jnp.float32)
        return (x, src, dst, edge_attr_3)
    x, src, dst, edge_attr_3 = _rec_inputs()

    def _L0_gnn_setup():
        import jax, jax.numpy as jnp
        import numpy as np
        N = 6250
        E = 50000
        IN = 256
        H = 8
        D = 32
        EF = 3
        key = jax.random.key(seed)
        ks = jax.random.split(key, 8)
        x = jax.random.normal(ks[0], (N, IN), dtype=jnp.float32)
        edge_index = jax.random.randint(ks[1], (2, E), 0, N, dtype=jnp.int64)
        edge_attr = jax.random.normal(ks[2], (E, EF), dtype=jnp.float32)
        W = jax.random.normal(ks[3], (H * D, IN), dtype=jnp.float32) * np.float32(np.sqrt(2.0 / (IN + H * D)))
        a_src = jax.random.normal(ks[4], (H, D), dtype=jnp.float32) * np.float32(np.sqrt(2.0 / (H + D)))
        a_dst = jax.random.normal(ks[5], (H, D), dtype=jnp.float32) * np.float32(np.sqrt(2.0 / (H + D)))
        edge_W = jax.random.normal(ks[6], (H * D, EF), dtype=jnp.float32) * np.float32(np.sqrt(2.0 / (EF + H * D)))
        edge_b = jnp.zeros((H * D,), dtype=jnp.float32)
        bias = jnp.zeros((H * D,), dtype=jnp.float32)
        return {'x': x, 'W': W, 'a_src': a_src, 'a_dst': a_dst, 'edge_W': edge_W, 'edge_b': edge_b, 'bias': bias, 'edge_attr': edge_attr, 'edge_index': edge_index}
    _L0_gnn_all = _L0_gnn_setup()
    _L0_gnn_in = {k: v for k, v in _L0_gnn_all.items() if k in ('W', 'a_src', 'a_dst', 'edge_W', 'edge_b', 'bias')}
    del _L0_gnn_all

    def _L0_mix_setup():
        import jax, jax.numpy as jnp
        import numpy as np
        A, Bc, Cc = (0.5, 1.0, 1.0)
        H = 8
        EPS = 1e-12

        def _normalize(t):
            n = jnp.linalg.norm(t, axis=-1, keepdims=True)
            return t / jnp.maximum(n, EPS)
        key = jax.random.key(seed)
        ks = jax.random.split(key, 5)
        B, N, C = (8, 256, 256)
        D = C // H
        x = jax.random.normal(ks[0], (B, N, C), dtype=jnp.float32)
        Wqkv = jax.random.normal(ks[1], (3 * H * D, C), dtype=jnp.float32) * 0.02
        bqkv = jnp.zeros((3 * H * D,), dtype=jnp.float32)
        Wproj = jax.random.normal(ks[2], (C, H * D), dtype=jnp.float32) * 0.02
        bproj = jnp.zeros((C,), dtype=jnp.float32)
        temperature = jnp.ones((1, H, 1, 1), dtype=jnp.float32)
        return {'x': x, 'Wqkv': Wqkv, 'bqkv': bqkv, 'Wproj': Wproj, 'bproj': bproj, 'temperature': temperature}
    _L0_mix_all = _L0_mix_setup()
    _L0_mix_in = {k: v for k, v in _L0_mix_all.items() if k in ('Wqkv', 'bqkv', 'Wproj', 'bproj', 'temperature')}
    del _L0_mix_all

    def _L0_ffn_setup():
        import jax, jax.numpy as jnp
        import numpy as np
        BN_EPS = 0.001

        def _bn(h, g, b, m, v):
            return g * (h - m) * jax.lax.rsqrt(v + BN_EPS) + b
        key = jax.random.key(seed)
        ks = jax.random.split(key, 8)
        B, F, Df = (256, 64, 256)
        E, H, D = (8, 256, 256)
        s1 = 1.0 / np.sqrt(Df)
        s2 = 1.0 / np.sqrt(H)
        return {'x': jax.random.normal(ks[0], (B, F, Df), jnp.float32), 'Wr': jax.random.normal(ks[1], (Df, E), jnp.float32) * s1, 'br': jnp.zeros((E,), jnp.float32), 'W1': jax.random.normal(ks[2], (E, Df, H), jnp.float32) * s1, 'b1': jnp.zeros((E, H), jnp.float32), 'g1': jnp.ones((E, H), jnp.float32), 'be1': jnp.zeros((E, H), jnp.float32), 'm1': jnp.zeros((E, H), jnp.float32), 'v1': jnp.ones((E, H), jnp.float32), 'W2': jax.random.normal(ks[3], (E, H, H), jnp.float32) * s2, 'b2': jnp.zeros((E, H), jnp.float32), 'g2': jnp.ones((E, H), jnp.float32), 'be2': jnp.zeros((E, H), jnp.float32), 'm2': jnp.zeros((E, H), jnp.float32), 'v2': jnp.ones((E, H), jnp.float32), 'Wo': jax.random.normal(ks[4], (E, H, D), jnp.float32) * s2, 'bo': jnp.zeros((E, D), jnp.float32)}
    _L0_ffn_all = _L0_ffn_setup()
    _L0_ffn_in = {k: v for k, v in _L0_ffn_all.items() if k in ('Wr', 'br', 'W1', 'b1', 'g1', 'be1', 'm1', 'v1', 'W2', 'b2', 'g2', 'be2', 'm2', 'v2', 'Wo', 'bo')}
    del _L0_ffn_all
    return {'x': x, 'src': src, 'dst': dst, 'edge_attr_3': edge_attr_3, 'L0_gnn_W': _L0_gnn_in['W'], 'L0_gnn_a_src': _L0_gnn_in['a_src'], 'L0_gnn_a_dst': _L0_gnn_in['a_dst'], 'L0_gnn_edge_W': _L0_gnn_in['edge_W'], 'L0_gnn_edge_b': _L0_gnn_in['edge_b'], 'L0_gnn_bias': _L0_gnn_in['bias'], 'L0_mix_Wqkv': _L0_mix_in['Wqkv'], 'L0_mix_bqkv': _L0_mix_in['bqkv'], 'L0_mix_Wproj': _L0_mix_in['Wproj'], 'L0_mix_bproj': _L0_mix_in['bproj'], 'L0_mix_temperature': _L0_mix_in['temperature'], 'L0_ffn_Wr': _L0_ffn_in['Wr'], 'L0_ffn_br': _L0_ffn_in['br'], 'L0_ffn_W1': _L0_ffn_in['W1'], 'L0_ffn_b1': _L0_ffn_in['b1'], 'L0_ffn_g1': _L0_ffn_in['g1'], 'L0_ffn_be1': _L0_ffn_in['be1'], 'L0_ffn_m1': _L0_ffn_in['m1'], 'L0_ffn_v1': _L0_ffn_in['v1'], 'L0_ffn_W2': _L0_ffn_in['W2'], 'L0_ffn_b2': _L0_ffn_in['b2'], 'L0_ffn_g2': _L0_ffn_in['g2'], 'L0_ffn_be2': _L0_ffn_in['be2'], 'L0_ffn_m2': _L0_ffn_in['m2'], 'L0_ffn_v2': _L0_ffn_in['v2'], 'L0_ffn_Wo': _L0_ffn_in['Wo'], 'L0_ffn_bo': _L0_ffn_in['bo']}

def reference(x, src, dst, edge_attr_3, L0_gnn_W, L0_gnn_a_src, L0_gnn_a_dst, L0_gnn_edge_W, L0_gnn_edge_b, L0_gnn_bias, L0_mix_Wqkv, L0_mix_bqkv, L0_mix_Wproj, L0_mix_bproj, L0_mix_temperature, L0_ffn_Wr, L0_ffn_br, L0_ffn_W1, L0_ffn_b1, L0_ffn_g1, L0_ffn_be1, L0_ffn_m1, L0_ffn_v1, L0_ffn_W2, L0_ffn_b2, L0_ffn_g2, L0_ffn_be2, L0_ffn_m2, L0_ffn_v2, L0_ffn_Wo, L0_ffn_bo):
    import jax
    import jax.numpy as jnp

    def _L0_gnn_ref(x, W, a_src, a_dst, edge_W, edge_b, bias, edge_attr, edge_index):
        import jax, jax.numpy as jnp
        import numpy as np
        N = 6250
        E = 50000
        IN = 256
        H = 8
        D = 32
        EF = 3
        n = x.shape[0]
        h = (x @ W.T).reshape(n, H, D)
        src, dst = (edge_index[0], edge_index[1])
        h_src = h[src]
        h_dst = h[dst]
        alpha = jnp.einsum('ehd,hd->eh', h_src, a_src) + jnp.einsum('ehd,hd->eh', h_dst, a_dst)
        enc = jax.nn.relu(edge_attr @ edge_W.T + edge_b).reshape(-1, H, D)
        alpha = alpha + jnp.sum(enc * h_dst, axis=-1)
        alpha = jnp.where(alpha >= 0, alpha, 0.2 * alpha)
        amax = jax.ops.segment_max(alpha, dst, num_segments=n)
        ex = jnp.exp(alpha - amax[dst])
        denom = jax.ops.segment_sum(ex, dst, num_segments=n)
        attn = ex / jnp.maximum(denom[dst], 1e-10)
        out = jax.ops.segment_sum(h_src * attn[..., None], dst, num_segments=n)
        return out.reshape(n, H * D) + bias

    def _L0_mix_ref(x, Wqkv, bqkv, Wproj, bproj, temperature):
        import jax, jax.numpy as jnp
        import numpy as np
        A, Bc, Cc = (0.5, 1.0, 1.0)
        H = 8
        EPS = 1e-12

        def _normalize(t):
            n = jnp.linalg.norm(t, axis=-1, keepdims=True)
            return t / jnp.maximum(n, EPS)
        B, N, C = x.shape
        D = C // H
        scale = float(D) ** 0.25
        qkv = (x @ Wqkv.T + bqkv).reshape(B, N, 3, H, D)
        qkv = jnp.transpose(qkv, (2, 0, 3, 1, 4))
        q, k, v = (qkv[0], qkv[1], qkv[2])
        q = q * scale
        v1 = jnp.concatenate([jnp.ones((B, H, N, 1), dtype=v.dtype), v], axis=-1)
        qn = _normalize(q) * (scale * temperature)
        kn = _normalize(k) * scale
        vN = v1 / N
        kv_mod = jnp.einsum('bhni,bhnj,bhne->bhije', kn, kn, vN)
        kv = jnp.einsum('bhnd,bhne->bhde', kn, vN)
        vsum = jnp.sum(vN, axis=-2)[:, :, None, :]
        y = A * jnp.einsum('bhni,bhnj,bhije->bhne', qn, qn, kv_mod) + scale ** 2 * Bc * jnp.einsum('bhnd,bhde->bhne', qn, kv) + scale ** 4 * Cc * vsum
        y_norm, y = (y[..., :1], y[..., 1:])
        y = y / y_norm
        out = jnp.transpose(y, (0, 2, 1, 3)).reshape(B, N, H * D)
        return out @ Wproj.T + bproj

    def _L0_ffn_ref(x, Wr, br, W1, b1, g1, be1, m1, v1, W2, b2, g2, be2, m2, v2, Wo, bo):
        import jax, jax.numpy as jnp
        import numpy as np
        BN_EPS = 0.001

        def _bn(h, g, b, m, v):
            return g * (h - m) * jax.lax.rsqrt(v + BN_EPS) + b
        feat = jnp.mean(x, axis=0)
        w = jax.nn.softmax(feat @ Wr + br, axis=-1)
        h = jnp.einsum('bfd,edh->bfeh', x, W1) + b1
        h = jax.nn.relu(_bn(h, g1, be1, m1, v1))
        h = jnp.einsum('bfeh,ehk->bfek', h, W2) + b2
        h = jax.nn.relu(_bn(h, g2, be2, m2, v2))
        y = jnp.einsum('bfeh,ehd->bfed', h, Wo) + bo
        return jnp.einsum('bfed,fe->bfd', y, w)
    edge_index = jnp.stack([src, dst])
    xn = _layernorm(x, axis=-1)
    x = x + _L0_gnn_ref(xn, L0_gnn_W, L0_gnn_a_src, L0_gnn_a_dst, L0_gnn_edge_W, L0_gnn_edge_b, L0_gnn_bias, edge_attr_3, edge_index) + _L0_mix_ref(xn[None], L0_mix_Wqkv, L0_mix_bqkv, L0_mix_Wproj, L0_mix_bproj, L0_mix_temperature)[0]
    x = x + _L0_ffn_ref(_layernorm(x, axis=-1)[None], L0_ffn_Wr, L0_ffn_br, L0_ffn_W1, L0_ffn_b1, L0_ffn_g1, L0_ffn_be1, L0_ffn_m1, L0_ffn_v1, L0_ffn_W2, L0_ffn_b2, L0_ffn_g2, L0_ffn_be2, L0_ffn_m2, L0_ffn_v2, L0_ffn_Wo, L0_ffn_bo)[0]
    return x

_drawn_inputs = setup_inputs


def setup_inputs(seed=0):
    import zlib

    import numpy as np

    out = dict(_drawn_inputs(seed))
    spreads = {'L0_gnn_edge_b': (0.0, 0.1),
     'L0_gnn_bias': (0.0, 0.1),
     'L0_mix_bqkv': (0.0, 0.286),
     'L0_mix_bproj': (0.0, 0.1),
     'L0_mix_temperature': (1.0, 0.6),
     'L0_ffn_br': (0.0, 0.1),
     'L0_ffn_b1': (0.0, 0.344),
     'L0_ffn_g1': (1.0, 0.2),
     'L0_ffn_be1': (0.0, 0.342),
     'L0_ffn_m1': (0.0, 0.333),
     'L0_ffn_v1': (1.0, 0.6),
     'L0_ffn_b2': (0.0, 0.1),
     'L0_ffn_g2': (1.0, 0.2),
     'L0_ffn_be2': (0.0, 0.1),
     'L0_ffn_m2': (0.0, 0.1),
     'L0_ffn_v2': (1.0, 0.6),
     'L0_ffn_bo': (0.0, 0.1)}
    factors = {'L0_mix_Wqkv': 30.338}
    for name, (base, spread) in spreads.items():
        noise = np.random.default_rng([zlib.crc32(name.encode()), seed]).standard_normal(out[name].shape)
        drawn = base * np.exp(spread * noise) if base else spread * noise
        out[name] = jnp.asarray(drawn.astype(out[name].dtype))
    for name, factor in factors.items():
        out[name] = (out[name] * factor).astype(out[name].dtype)
    return out
```

```python
import numpy as np
import concourse.bass as bass
import concourse.mybir as mybir
from contextlib import ExitStack

F32 = mybir.dt.float32
BF16 = mybir.dt.bfloat16
I32 = mybir.dt.int32
ALU = mybir.AluOpType
ACT = mybir.ActivationFunctionType
AX = mybir.AxisListType.X

P = 128
C = 256
H = 8
HD = C // H
EXPERTS = 8
LN_EPS = 1e-5
NORM_EPS = 1e-12
BN_EPS = 1e-3
DEN_MIN = 1e-10
SLOPE = 0.2
QK_SCALE = float(HD) ** 0.25

AUG = HD + 1
TURNS = AUG // 2 + 1
EXT = AUG + TURNS - 1
PAIRS = TURNS * AUG
PB = -(-PAIRS // P)
VE = HD + 1
POOL_HEADS = 2
SRC_W = H + C
DST_W = C + H
ALL_W = H + C + H
TG = 4
GE = TG * P
NEG = -3.0e38


def wait(eng, sem, value):
    if not (isinstance(value, int) and value <= 0):
        eng.wait_ge(sem, value)


def ready(eng, sem, k, u, inc=1):
    wait(eng, sem[u], inc * (k + 1))


def freed(eng, sem, k, u, inc=1):
    wait(eng, sem[u], inc * k)


def before(eng, sem, k, u, inc=1):
    if u == 0:
        wait(eng, sem[1], inc * k)
    else:
        wait(eng, sem[0], inc * (k + 1))


def turns(eng, n, body):
    body(0)
    if n > 1:
        with eng.Fori(1, n) as k:
            body(k)


def pairs(eng, n, body):
    def two(k):
        body(2 * k, k, 0)
        body(2 * k + 1, k, 1)

    turns(eng, n // 2, two)
    if n % 2:
        body(n - 1, n // 2, 0)


def skewed(eng, n, ahead, body):
    def two(k):
        ahead(2 * k + 1, k, 1)
        body(2 * k, k, 0)
        ahead(2 * k + 2, k + 1, 0)
        body(2 * k + 1, k, 1)

    ahead(0, 0, 0)
    half = (n - 1) // 2
    turns(eng, half, two)
    if n % 2 == 0:
        ahead(n - 1, half, 1)
        body(n - 2, half, 0)
        body(n - 1, half, 1)
    else:
        body(n - 1, half, 0)


class Kit:

    def __init__(self, nc, stack, tag=""):
        self.nc, self.stack, self.tag, self.sems = nc, stack, tag, []

    def sb(self, name, shape, dt=F32):
        return self.stack.enter_context(self.nc.sbuf_tensor(self.tag + name, shape, dt))

    def ps(self, name, shape, dt=F32):
        return self.stack.enter_context(self.nc.psum_tensor(self.tag + name, shape, dt))

    def sem(self, name):
        self.sems.append(self.nc.alloc_semaphore(self.tag + name))
        return self.sems[-1]

    def free(self):
        self.nc.clear_and_free_semaphores(self.sems)
        self.nc.all_engine_barrier()

    def sem2(self, name):
        return [self.sem(f"{name}_{u}") for u in range(2)]


def row(d, i):
    return d[bass.ds(i, 1)]


def stage_constants(nc, g, dims, ins, keep):
    NT, N = dims["NT"], dims["N"]
    with ExitStack() as st:
        s = Kit(nc, st, "c_")
        w_nat = s.sb("w_nat", [P, 2, C])
        a_blk = s.sb("a_blk", [P, 2, 2 * H])
        stats = s.sb("stats", [P, NT, 6])
        t0 = s.sb("t0", [P, NT])
        t1 = s.sb("t1", [P, NT])
        mean = s.sb("mean", [P, NT])
        var = s.sb("var", [P, NT])
        ones = s.sb("ones", [P, P])
        iota_i = s.sb("iota_i", [P, P], I32)
        iota_pi = s.sb("iota_pi", [P, 1], I32)
        ps_fold = s.ps("ps_fold", [P, 2, 2 * H])
        x_in = s.sem("x_in")
        w_in = s.sem("w_in")
        ones_set = s.sem("ones_set")
        consts_made = s.sem("consts_made")
        folded = s.sem("folded")
        fold_put = s.sem("fold_put")
        stats_made = s.sem("stats_made")
        step = s.sem("step")
        var_made = s.sem("var_made")
        std_made = s.sem("std_made")
        with nc.Block() as block:
            @block.sync
            def _(sp):
                sp.dma_start(w_nat[:], ins["w_nat"]).then_inc(w_in, 16)
                sp.dma_start(a_blk[:], ins["a_blk"]).then_inc(w_in, 16)
                sp.dma_start(keep["x_all"][:], ins["x"]).then_inc(x_in, 16)
                sp.dma_start(keep["w_h"][:, :, H:H + C], ins["w_t"]).then_inc(w_in, 16)
                sp.dma_start(keep["w_qkv"][:], ins["w_qkv_t"]).then_inc(w_in, 16)
                sp.dma_start(keep["b_qkv"][:], ins["b_qkv"].partition_broadcast(P)).then_inc(w_in, 16)
                sp.dma_start(keep["w_proj"][:], ins["w_proj_t"]).then_inc(w_in, 16)
                sp.dma_start(keep["b_res"][:, 0, :], ins["b_proj"].partition_broadcast(P)).then_inc(w_in, 16)
                sp.dma_start(keep["b_res"][:, 1, :], ins["gnn_bias"].partition_broadcast(P)).then_inc(w_in, 16)
                sp.dma_start(keep["c_out"][:, 0:H], ins["temp"].partition_broadcast(P)).then_inc(w_in, 16)

            @block.gpsimd
            def _(pool):
                nc.gpsimd.memset(keep["ident"][:], 0.0).then_inc(ones_set, 1)
                pool.wait_ge(ones_set, 1)
                nc.gpsimd.affine_select(out=keep["ident"][:], in_=keep["ident"][:], compare_op=ALU.not_equal,
                                        fill=1.0, base=0, pattern=[[-1, P]], channel_multiplier=1).then_inc(consts_made, 1)
                nc.gpsimd.iota(iota_i[:], pattern=[[1, P]], base=0, channel_multiplier=0).then_inc(consts_made, 1)
                nc.gpsimd.iota(iota_pi[:], pattern=[[1, 1]], base=0, channel_multiplier=1).then_inc(consts_made, 1)

            @block.tensor
            def _(pe):
                pe.wait_ge(w_in, 16 * 9)
                for half in range(2):
                    for q in range(2):
                        last = nc.tensor.matmul(ps_fold[:, half, :], w_nat[:, q, half * P:(half + 1) * P],
                                                a_blk[:, q, :], start=(q == 0), stop=(q == 1))
                last.then_inc(folded, 1)

            @block.scalar
            def _(act):
                act.wait_ge(var_made, 1)
                nc.scalar.activation(t1[:], var[:], ACT.Sqrt).then_inc(std_made, 1)

            @block.vector
            def _(dve):
                n = [0]

                def link(ins_):
                    n[0] += 1
                    ins_.then_inc(step, 1)
                    dve.wait_ge(step, n[0])

                nc.vector.memset(keep["c_in"][:, 0:H], QK_SCALE ** 2)
                nc.vector.memset(keep["c_in"][:, H:2 * H], 1.0)
                link(nc.vector.memset(keep["c_out"][:, H:2 * H], QK_SCALE))
                dve.wait_ge(consts_made, 3)
                link(nc.vector.tensor_copy(keep["iota_row"][:], iota_i[:]))
                link(nc.vector.tensor_copy(keep["iota_p"][:], iota_pi[:]))
                link(nc.vector.tensor_scalar(keep["in_range"][:], keep["iota_p"][:], float(N - (NT - 1) * P), None, ALU.is_lt))
                link(nc.vector.tensor_scalar(keep["c_pair"][:], keep["iota_p"][:], float(HD), -0.5 / N, ALU.is_lt, ALU.mult))
                link(nc.vector.tensor_scalar(keep["c_pair"][:], keep["c_pair"][:], 1.0 / N, None, ALU.add))
                dve.wait_ge(w_in, 16 * 9)
                link(nc.vector.tensor_scalar(keep["c_out"][:, 0:H], keep["c_out"][:, 0:H], QK_SCALE ** 2, None, ALU.mult))
                link(nc.vector.tensor_tensor(keep["b_res"][:, 0, :], keep["b_res"][:, 0, :], keep["b_res"][:, 1, :], ALU.add))
                dve.wait_ge(folded, 1)
                nc.vector.tensor_copy(keep["w_h"][:, :, 0:H], ps_fold[:, :, 0:H])
                link(nc.vector.tensor_copy(keep["w_h"][:, :, H + C:ALL_W], ps_fold[:, :, H:2 * H]))
                dve.wait_ge(x_in, 16)
                with dve.Fori(0, NT) as i:
                    nc.vector.bn_stats(stats[:, bass.ds(i, 1), :], keep["x_all"][:, bass.ds(i, 1), :]).then_inc(stats_made, 1)
                dve.wait_ge(stats_made, NT)
                link(nc.vector.tensor_tensor(t0[:], stats[:, :, 1], stats[:, :, 4], ALU.add))
                link(nc.vector.tensor_scalar(mean[:], t0[:], 0.5, None, ALU.mult))
                link(nc.vector.tensor_tensor(t0[:], stats[:, :, 1], stats[:, :, 4], ALU.subtract))
                link(nc.vector.tensor_tensor(t0[:], t0[:], t0[:], ALU.mult))
                link(nc.vector.tensor_scalar(t0[:], t0[:], 0.25, LN_EPS, ALU.mult, ALU.add))
                link(nc.vector.tensor_tensor(var[:], stats[:, :, 2], stats[:, :, 5], ALU.add))
                nc.vector.scalar_tensor_tensor(out=var[:], in0=var[:], scalar=1.0 / C, in1=t0[:], op0=ALU.mult,
                                               op1=ALU.add).then_inc(var_made, 1)
                dve.wait_ge(std_made, 1)
                link(nc.vector.reciprocal(keep["rstd"][:], t1[:]))
                link(nc.vector.scalar_tensor_tensor(out=keep["nmr"][:], in0=mean[:], scalar=-1.0, in1=keep["rstd"][:],
                                                    op0=ALU.mult, op1=ALU.mult))
        s.free()


def turned(t, u, heads, repeat):
    h0, h1 = heads
    a = t[:, u, h0:h1, :]
    return bass.AP(a.tensor, a.offset, [a.ap[0], [EXT, h1 - h0], [0 if repeat else 1, TURNS], [1, AUG]])


def stage_nodes(nc, g, dims, ins, keep, scr):
    NT, N = dims["NT"], dims["N"]
    with ExitStack() as st:
        s = Kit(nc, st, "n_")
        xn = s.sb("xn", [P, 2, C])
        xnT = s.sb("xnT", [P, 2, 2, P])
        hs = s.sb("hs", [P, 2, ALL_W])
        parts = s.sb("parts", [P, 2, 3, DST_W], BF16)
        rest = s.sb("rest", [P, 2, DST_W])
        qk = s.sb("qk", [P, 2, 2 * C])
        sq = s.sb("sq", [P, 2, 2 * C])
        ssq = s.sb("ssq", [P, 2, 2 * H])
        nrm = s.sb("nrm", [P, 2, 2 * H])
        fac = s.sb("fac", [P, 2, 2 * H])
        vv = s.sb("vv", [P, 2, H, VE])
        q2 = s.sb("q2", [P, 2, H, EXT])
        k2 = s.sb("k2", [P, 2, H, EXT])
        prod = s.sb("prod", [P, 2, H, PB * P])
        zeros = s.sb("zeros", [P, 512])
        ps_t = s.ps("ps_t", [P, 2, P])
        ps_h = s.ps("ps_h", [P, 512])
        ps_qk = s.ps("ps_qk", [P, 512])
        ps_v = s.ps("ps_v", [P, C])
        GB = 15
        ps_g = [s.ps(f"ps_g{b}", [P, 512]) for b in range(3)]

        set_up = s.sem("set_up")
        pool_up = s.sem("pool_up")
        xn_made = s.sem2("xn_made")
        xt_done = s.sem2("xt_done")
        xnT_made = s.sem2("xnT_made")
        proj_done = s.sem2("proj_done")
        hs_made = s.sem2("hs_made")
        part0 = s.sem2("part0")
        rest1 = s.sem2("rest1")
        part1 = s.sem2("part1")
        part2 = s.sem2("part2")
        qk_made = s.sem2("qk_made")
        vv_made = s.sem2("vv_made")
        sq_made = s.sem2("sq_made")
        ssq_raw = s.sem2("ssq_raw")
        ssq_made = s.sem2("ssq_made")
        nrm_made = s.sem2("nrm_made")
        nrm_held = s.sem2("nrm_held")
        fac_raw = s.sem2("fac_raw")
        fac_made = s.sem2("fac_made")
        q_scaled = s.sem2("q_scaled")
        q_made = s.sem2("q_made")
        k_scaled = s.sem2("k_scaled")
        k_made = s.sem2("k_made")
        prod_dve = s.sem2("prod_dve")
        prod_pool = s.sem2("prod_pool")
        summed = s.sem2("summed")
        h_stored = s.sem2("h_stored")
        d_stored = s.sem2("d_stored")
        q_stored = s.sem2("q_stored")
        masked = s.sem("masked")

        with nc.Block() as block:
            @block.scalar
            def _(act):
                def normalise(i, k, u):
                    freed(act, xt_done, k, u)
                    nc.scalar.activation(xn[:, u, :], keep["x_all"][:, bass.ds(i, 1), :], ACT.Identity,
                                         scale=keep["rstd"][:, bass.ds(i, 1)], bias=keep["nmr"][:, bass.ds(i, 1)]).then_inc(xn_made[u], 1)
                    ready(act, xt_done, k, u)
                    freed(act, proj_done, k, u)
                    nc.scalar.copy(xnT[:, u], ps_t[:]).then_inc(xnT_made[u], 1)

                def rest_of(i, k, u):
                    ready(act, proj_done, k, u)
                    freed(act, h_stored, k, u, 16)
                    freed(act, rest1, k, u)
                    nc.scalar.copy(hs[:, u, :], ps_h[:, 0:ALL_W]).then_inc(hs_made[u], 1)
                    ready(act, hs_made, k, u)
                    freed(act, d_stored, k, u, 16)
                    nc.scalar.copy(parts[:, u, 0, :], hs[:, u, H:ALL_W]).then_inc(part0[u], 1)
                    ready(act, qk_made, k, u)
                    freed(act, ssq_raw, k, u)
                    nc.scalar.activation(sq[:, u, :], qk[:, u, :], ACT.Square).then_inc(sq_made[u], 1)
                    ready(act, ssq_made, k, u)
                    freed(act, nrm_held, k, u)
                    nc.scalar.activation(nrm[:, u, :], ssq[:, u, :], ACT.Sqrt).then_inc(nrm_made[u], 1)

                skewed(act, NT, normalise, rest_of)

            @block.tensor
            def _(pe):
                pe.wait_ge(set_up, 1)
                for b in range(3):
                    nc.tensor.matmul(ps_g[b][:], zeros[:, 0:P], zeros[:], start=True, stop=True, skip_group_check=True)

                def project(i, k, u):
                    ready(pe, xn_made, k, u)
                    before(pe, xnT_made, k, u)
                    for c in range(2):
                        last = nc.tensor.transpose(ps_t[:, c, :], xn[:, u, c * P:(c + 1) * P], keep["ident"][:])
                    last.then_inc(xt_done[u], 1)
                    ready(pe, xnT_made, k, u)
                    before(pe, hs_made, k, u)
                    before(pe, qk_made, k, u)
                    before(pe, vv_made, k, u)
                    for out, w in ((ps_h[:, 0:ALL_W], keep["w_h"][:, :, :]), (ps_qk[:], keep["w_qkv"][:, :, 0:2 * C]),
                                   (ps_v[:], keep["w_qkv"][:, :, 2 * C:3 * C])):
                        for c in range(2):
                            last = nc.tensor.matmul(out, xnT[:, u, c, :], w[:, c, :], start=(c == 0), stop=(c == 1))
                    last.then_inc(proj_done[u], 1)

                def sum_products(i, k, u):
                    ready(pe, vv_made, k, u)
                    if isinstance(i, int) and i == NT - 1:
                        pe.wait_ge(masked, 1)
                    for h in range(H):
                        if h == 0:
                            ready(pe, prod_dve, k, u)
                        if h == H - POOL_HEADS:
                            ready(pe, prod_pool, k, u)
                        for b in range(PB):
                            c = h * PB + b
                            last = nc.tensor.matmul(ps_g[c // GB][:, (c % GB) * VE:(c % GB + 1) * VE],
                                                    prod[:, u, h, b * P:(b + 1) * P], vv[:, u, h, :],
                                                    start=False, stop=True, skip_group_check=True)
                    last.then_inc(summed[u], 1)

                skewed(pe, NT, project, sum_products)

            @block.vector
            def _(dve):
                nc.vector.memset(vv[:, :, :, 0:1], 1.0)
                nc.vector.memset(q2[:, :, :, HD:AUG], QK_SCALE)
                nc.vector.memset(k2[:, :, :, HD:AUG], QK_SCALE)
                nc.vector.memset(prod[:, :, :, PAIRS:PB * P], 0.0)
                nc.vector.memset(zeros[:], 0.0).then_inc(set_up, 1)
                dve.wait_ge(set_up, 1)

                def body(i, k, u):
                    ready(dve, proj_done, k, u)
                    freed(dve, q_scaled, k, u)
                    freed(dve, k_scaled, k, u)
                    freed(dve, sq_made, k, u)
                    nc.vector.tensor_tensor(qk[:, u, :], ps_qk[:], keep["b_qkv"][:, 0:2 * C], ALU.add).then_inc(qk_made[u], 1)
                    freed(dve, summed, k, u)
                    nc.vector.tensor_tensor(vv[:, u, :, 1:VE], ps_v[:].rearrange("p (h d) -> p h d", h=H),
                                            keep["b_qkv"][:, 2 * C:3 * C].rearrange("p (h d) -> p h d", h=H),
                                            ALU.add).then_inc(vv_made[u], 1)
                    if isinstance(i, int) and i == NT - 1:
                        ready(dve, vv_made, k, u)
                        nc.vector.tensor_scalar(vv[:, u], vv[:, u], keep["in_range"][:, 0:1], None, ALU.mult).then_inc(masked, 1)
                    ready(dve, part0, k, u)
                    freed(dve, part2, k, u)
                    nc.vector.tensor_tensor(rest[:, u, :], hs[:, u, H:ALL_W], parts[:, u, 0, :], ALU.subtract).then_inc(rest1[u], 1)
                    ready(dve, sq_made, k, u)
                    freed(dve, nrm_made, k, u)
                    nc.vector.reduce_sum(ssq[:, u, :], sq[:, u, :].rearrange("p (h d) -> p h d", d=HD), AX).then_inc(ssq_raw[u], 1)
                    ready(dve, rest1, k, u)
                    nc.vector.tensor_copy(parts[:, u, 1, :], rest[:, u, :]).then_inc(part1[u], 1)
                    ready(dve, ssq_raw, k, u)
                    nc.vector.tensor_tensor(ssq[:, u, :], ssq[:, u, :], keep["c_in"][:], ALU.mult).then_inc(ssq_made[u], 1)
                    ready(dve, part1, k, u)
                    nc.vector.tensor_tensor(parts[:, u, 2, :], rest[:, u, :], parts[:, u, 1, :], ALU.subtract).then_inc(part2[u], 1)
                    ready(dve, nrm_made, k, u)
                    nc.vector.tensor_scalar(fac[:, u, :], nrm[:, u, :], NORM_EPS, None, ALU.max).then_inc(nrm_held[u], 1)
                    ready(dve, nrm_held, k, u)
                    nc.vector.reciprocal(fac[:, u, :], fac[:, u, :]).then_inc(fac_raw[u], 1)
                    ready(dve, fac_raw, k, u)
                    nc.vector.tensor_tensor(fac[:, u, :], fac[:, u, :], keep["c_out"][:], ALU.mult).then_inc(fac_made[u], 1)
                    ready(dve, fac_made, k, u)
                    freed(dve, prod_pool, k, u)
                    for which, dst, scaled in ((1, k2, k_scaled), (0, q2, q_scaled)):
                        if which == 0:
                            freed(dve, q_stored, k, u, 16)
                        nc.vector.tensor_tensor(dst[:, u, :, 0:HD],
                                                qk[:, u, which * C:(which + 1) * C].rearrange("p (h d) -> p h d", h=H),
                                                fac[:, u, which * H:(which + 1) * H].unsqueeze(2).to_broadcast([P, H, HD]),
                                                ALU.mult).then_inc(scaled[u], 1)
                    ready(dve, k_scaled, k, u)
                    nc.vector.tensor_copy(k2[:, u, :, AUG:EXT], k2[:, u, :, 0:TURNS - 1]).then_inc(k_made[u], 1)
                    ready(dve, q_scaled, k, u)
                    nc.vector.tensor_copy(q2[:, u, :, AUG:EXT], q2[:, u, :, 0:TURNS - 1]).then_inc(q_made[u], 1)
                    ready(dve, k_made, k, u)
                    hv = (0, H - POOL_HEADS)
                    nc.vector.tensor_tensor(prod[:, u, hv[0]:hv[1], 0:PAIRS].rearrange("p h (r i) -> p h r i", i=AUG),
                                            turned(k2, u, hv, True), turned(k2, u, hv, False), ALU.mult).then_inc(prod_dve[u], 1)

                pairs(dve, NT, body)
                ready(dve, summed, NT // 2, 0)
                for h in range(H):
                    for b in range(PB):
                        c = h * PB + b
                        src = ps_g[c // GB][:, (c % GB) * VE:(c % GB + 1) * VE]
                        w = keep["c_pair"][:, 0:1] if b == 0 else 1.0 / N
                        nc.vector.tensor_scalar(keep["g_sum"][:, c, :], src, w, None, ALU.mult)

            @block.gpsimd
            def _(pool):
                pool.wait_ge(set_up, 1)

                def body(i, k, u):
                    ready(pool, hs_made, k, u)
                    pool.dma_start(row(scr["src_rows"], i).rearrange("o p w -> p (o w)"), hs[:, u, 0:SRC_W]).then_inc(h_stored[u], 16)
                    ready(pool, part2, k, u)
                    pool.dma_start(row(scr["dst_parts"], i).rearrange("o p w -> p (o w)"),
                                   parts[:, u].rearrange("p a w -> p (a w)")).then_inc(d_stored[u], 16)
                    ready(pool, k_made, k, u)
                    freed(pool, summed, k, u)
                    hv = (H - POOL_HEADS, H)
                    nc.gpsimd.tensor_tensor(prod[:, u, hv[0]:hv[1], 0:PAIRS].rearrange("p h (r i) -> p h r i", i=AUG),
                                            turned(k2, u, hv, True), turned(k2, u, hv, False), ALU.mult).then_inc(prod_pool[u], 1)
                    ready(pool, q_made, k, u)
                    pool.dma_start(row(scr["q_rows"], i).rearrange("o p w -> p (o w)"),
                                   q2[:, u].rearrange("p h e -> p (h e)")).then_inc(q_stored[u], 16)

                pairs(pool, NT, body)
                for sem in (h_stored, d_stored, q_stored):
                    pool.wait_ge(sem[0], 16 * (NT // 2 + 1))
                    pool.wait_ge(sem[1], 16 * (NT // 2))
        s.free()


def stage_mix(nc, g, dims, ins, keep, scr):
    NT = dims["NT"]
    with ExitStack() as st:
        s = Kit(nc, st, "m_")
        q2 = s.sb("q2", [P, 2, H, EXT])
        prod = s.sb("prod", [P, 2, H, PB * P])
        prodT = s.sb("prodT", [P, 2, PB, P])
        ry = s.sb("ry", [P, 2, H])
        yn = s.sb("yn", [P, 2, C])
        ynT = s.sb("ynT", [P, 2, 2, P])
        xb = s.sb("xb", [P, 2, C])
        res = s.sb("res", [P, 2, C])
        ps_p = [s.ps(f"ps_p{b}", [P, 8, P]) for b in range(2)]
        ps_y = s.ps("ps_y", [P, H, VE])
        ps_yt = s.ps("ps_yt", [P, 2, P])
        ps_o = s.ps("ps_o", [P, C])
        set_up = s.sem("set_up")
        q_in = s.sem2("q_in")
        prod_dve = s.sem2("prod_dve")
        prod_pool = s.sem2("prod_pool")
        turned_t = s.sem2("turned_t")
        prodT_made = s.sem2("prodT_made")
        head_done = s.sem2("head_done")
        ry_made = s.sem2("ry_made")
        yn_made = s.sem2("yn_made")
        yt_done = s.sem2("yt_done")
        ynT_made = s.sem2("ynT_made")
        o_done = s.sem2("o_done")
        xb_made = s.sem2("xb_made")
        res_made = s.sem2("res_made")
        res_stored = s.sem2("res_stored")
        HH = H // 2

        with nc.Block() as block:
            @block.sync
            def _(sp):
                def load(i, k, u):
                    freed(sp, prod_dve, k, u)
                    freed(sp, prod_pool, k, u)
                    sp.dma_start(q2[:, u].rearrange("p h e -> p (h e)"), row(scr["q_rows"], i).rearrange("o p w -> p (o w)")).then_inc(q_in[u], 16)

                def store(i, k, u):
                    ready(sp, res_made, k, u)
                    sp.dma_start(row(scr["x_mix"], i).rearrange("o p w -> p (o w)"), res[:, u, :]).then_inc(res_stored[u], 16)

                skewed(sp, NT, load, store)
                sp.wait_ge(res_stored[0], 16 * (NT // 2 + 1))
                sp.wait_ge(res_stored[1], 16 * (NT // 2))

            @block.gpsimd
            def _(pool):
                nc.gpsimd.memset(prod[:, :, :, PAIRS:PB * P], 0.0).then_inc(set_up, 1)

                def body(i, k, u):
                    ready(pool, q_in, k, u, 16)
                    freed(pool, yn_made, k, u)
                    hv = (H - POOL_HEADS, H)
                    nc.gpsimd.tensor_tensor(prod[:, u, hv[0]:hv[1], 0:PAIRS].rearrange("p h (r i) -> p h r i", i=AUG),
                                            turned(q2, u, hv, True), turned(q2, u, hv, False), ALU.mult).then_inc(prod_pool[u], 1)
                    freed(pool, res_made, k, u)
                    nc.gpsimd.tensor_tensor(xb[:, u, :], keep["x_all"][:, bass.ds(i, 1), :].rearrange("p o c -> p (o c)"),
                                            keep["b_res"][:, 0, :], ALU.add).then_inc(xb_made[u], 1)

                pairs(pool, NT, body)

            @block.vector
            def _(dve):
                def products(i, k, u):
                    ready(dve, q_in, k, u, 16)
                    freed(dve, yn_made, k, u)
                    hv = (0, H - POOL_HEADS)
                    nc.vector.tensor_tensor(prod[:, u, hv[0]:hv[1], 0:PAIRS].rearrange("p h (r i) -> p h r i", i=AUG),
                                            turned(q2, u, hv, True), turned(q2, u, hv, False), ALU.mult).then_inc(prod_dve[u], 1)

                def finish(i, k, u):
                    dve.wait_ge(head_done[1], HH * (i + 1))
                    freed(dve, yn_made, k, u)
                    nc.vector.reciprocal(ry[:, u, :], ps_y[:, :, 0]).then_inc(ry_made[u], 1)
                    ready(dve, ry_made, k, u)
                    freed(dve, yt_done, k, u)
                    nc.vector.tensor_tensor(yn[:, u, :].rearrange("p (h d) -> p h d", h=H), ps_y[:, :, 1:VE],
                                            ry[:, u, :].unsqueeze(2).to_broadcast([P, H, HD]), ALU.mult).then_inc(yn_made[u], 1)
                    ready(dve, o_done, k, u)
                    ready(dve, xb_made, k, u)
                    freed(dve, res_stored, k, u, 16)
                    nc.vector.tensor_tensor(res[:, u, :], ps_o[:], xb[:, u, :], ALU.add).then_inc(res_made[u], 1)

                skewed(dve, NT, products, finish)

            @block.scalar
            def _(act):
                def body(i, k, u):
                    for h in range(H):
                        n = HH * i + h // 2
                        act.wait_ge(turned_t[h % 2], n + 1)
                        wait(act, head_done[h % 2], n)
                        nc.scalar.copy(prodT[:, h % 2], ps_p[h % 2][:, 0:PB, :]).then_inc(prodT_made[h % 2], 1)
                    ready(act, yt_done, k, u)
                    freed(act, o_done, k, u)
                    nc.scalar.copy(ynT[:, u], ps_yt[:]).then_inc(ynT_made[u], 1)

                pairs(act, NT, body)

            @block.tensor
            def _(pe):
                pe.wait_ge(set_up, 1)

                def body(i, k, u):
                    def turn(h):
                        n = HH * i + h // 2
                        if h == 0:
                            ready(pe, prod_dve, k, u)
                        if h == H - POOL_HEADS:
                            ready(pe, prod_pool, k, u)
                        wait(pe, prodT_made[h % 2], n)
                        for b in range(PB):
                            last = nc.tensor.transpose(ps_p[h % 2][:, b, :], prod[:, u, h, b * P:(b + 1) * P], keep["ident"][:])
                        last.then_inc(turned_t[h % 2], 1)

                    def weigh(h):
                        n = HH * i + h // 2
                        pe.wait_ge(prodT_made[h % 2], n + 1)
                        if h == 0:
                            before(pe, yn_made, k, u)
                        for b in range(PB):
                            last = nc.tensor.matmul(ps_y[:, h, :], prodT[:, h % 2, b, :], keep["g_sum"][:, h * PB + b, :],
                                                    start=(b == 0), stop=(b == PB - 1))
                        last.then_inc(head_done[h % 2], 1)

                    turn(0)
                    for h in range(1, H):
                        turn(h)
                        weigh(h - 1)
                    weigh(H - 1)
                    ready(pe, yn_made, k, u)
                    for c in range(2):
                        last = nc.tensor.transpose(ps_yt[:, c, :], yn[:, u, c * P:(c + 1) * P], keep["ident"][:])
                    last.then_inc(yt_done[u], 1)
                    ready(pe, ynT_made, k, u)
                    before(pe, res_made, k, u)
                    for c in range(2):
                        last = nc.tensor.matmul(ps_o[:], ynT[:, u, c, :], keep["w_proj"][:, c, :], start=(c == 0), stop=(c == 1))
                    last.then_inc(o_done[u], 1)

                pairs(pe, NT, body)
        s.free()



def plan_dims(N, E):
    NT = -(-N // P)
    T = -(-E // GE)
    S = T + NT - 1
    S += (-S) % 4
    assert NT % 2 == 1 and NT % 7 == 0 and E < T * GE and S <= 512 and T <= 512
    return dict(N=N, E=E, NT=NT, T=T, S=S)


def lay_out(a):
    a = {n: np.asarray(v) for n, v in a.items()}
    N, E = a["x"].shape[0], a["src"].shape[0]
    d = plan_dims(N, E)
    NT, T = d["NT"], d["T"]

    def halves(w):
        return np.ascontiguousarray(w.reshape(2, P, -1).transpose(1, 0, 2))

    def cols(v):
        return np.ascontiguousarray(v.reshape(EXPERTS, 2, P).transpose(2, 0, 1))

    o = {}
    x = np.zeros((NT * P, C), np.float32)
    x[:N] = a["x"]
    o["x"] = np.ascontiguousarray(x.reshape(NT, P, C).transpose(1, 0, 2))
    blk = np.zeros((C, 2 * H), np.float32)
    for h in range(H):
        blk[h * HD:(h + 1) * HD, h] = a["L0_gnn_a_src"][h]
        blk[h * HD:(h + 1) * HD, H + h] = a["L0_gnn_a_dst"][h]
    o["a_blk"] = halves(blk)
    o["w_nat"] = halves(a["L0_gnn_W"])
    o["w_t"] = halves(a["L0_gnn_W"].T)
    o["w_qkv_t"] = halves(a["L0_mix_Wqkv"].T)
    o["b_qkv"] = a["L0_mix_bqkv"]
    o["w_proj_t"] = halves(a["L0_mix_Wproj"].T)
    o["b_proj"] = a["L0_mix_bproj"]
    o["gnn_bias"] = a["L0_gnn_bias"]
    o["temp"] = a["L0_mix_temperature"].reshape(H)
    dst = np.full(T * GE, 1 << 20, np.int32)
    dst[:E] = a["dst"]
    src = np.zeros(T * GE, np.int32)
    src[:E] = a["src"]
    prev = np.full(T * GE, -1, np.int32)
    prev[1:] = dst[:-1]
    o["dst_rows"] = np.concatenate([prev.reshape(T, GE)[:, :1], dst.reshape(T, GE)], axis=1)
    o["group_last"] = np.ascontiguousarray(dst.reshape(T, GE)[:, GE - 1:])
    o["src_in"] = src.reshape(T, GE)
    ea = np.zeros((T * GE, 4), np.float32)
    ea[:E, :3] = a["edge_attr_3"]
    ea[:, 3] = 1.0
    o["edge_t"] = np.ascontiguousarray(ea.reshape(T, GE, 4).transpose(0, 2, 1))
    o["w_edge"] = np.concatenate([a["L0_gnn_edge_W"].T, a["L0_gnn_edge_b"][None]], axis=0)
    for n in ("W1", "W2", "Wo"):
        o[n] = np.ascontiguousarray(a["L0_ffn_" + n].reshape(EXPERTS, 2, P, C).transpose(2, 0, 1, 3))
    for n in ("b1", "g1", "be1", "m1", "v1", "b2", "g2", "be2", "m2", "v2"):
        o[n] = cols(a["L0_ffn_" + n])
    o["Wr"] = halves(a["L0_ffn_Wr"])
    o["br"] = a["L0_ffn_br"]
    o["bo"] = a["L0_ffn_bo"]
    return o, d


def stage_plan(nc, dims, ins, keep, scr):
    NT, T, S = dims["NT"], dims["T"], dims["S"]
    TB = -(-T // P)
    SB = 4
    with ExitStack() as st:
        s = Kit(nc, st, "p_")
        steps_i = s.sb("steps_i", [P, GE], I32)
        steps = s.sb("steps", [P, GE])
        scol_i = s.sb("scol_i", [P, SB], I32)
        scol = s.sb("scol", [P, SB])
        ones = s.sb("ones", [P, P])
        last_i = s.sb("last_i", [P, TB], I32)
        last_f = s.sb("last_f", [P, TB])
        thr = s.sb("thr", [P, NT])
        less = s.sb("less", [P, TB, NT])
        f = s.sb("f", [NT, 1])
        f1 = s.sb("f1", [NT, 1])
        past = s.sb("past", [NT, GE])
        jrow = s.sb("jrow", [P, GE])
        trow = s.sb("trow", [1, GE])
        jcol = s.sb("jcol", [P, SB])
        j128 = s.sb("j128", [P, SB])
        tcol = s.sb("tcol", [P, SB])
        tcol_i = s.sb("tcol_i", [P, SB], I32)
        dst_g = s.sb("dst_g", [P, SB, GE + 1], I32)
        src_g = s.sb("src_g", [P, SB, GE], I32)
        rel = s.sb("rel", [P, SB, GE + 1])
        srcf = s.sb("srcf", [P, SB, GE])
        begin = s.sb("begin", [P, SB, GE])
        pen_b = s.sb("pen_b", [P, SB, GE], BF16)
        rel_b = s.sb("rel_b", [P, SB, GE], BF16)
        ps_e = s.ps("ps_e", [NT, 1])
        ps_l = s.ps("ps_l", [1, NT])
        ps_j = s.ps("ps_j", [P, GE])
        ps_jc = s.ps("ps_jc", [P, SB])
        ps_t = [s.ps(f"ps_t{u}", [P, TG, P]) for u in range(2)]
        l_in = s.sem("l_in")
        iotas = s.sem("iotas")
        step = s.sem("step")
        less_made = s.sem("less_made")
        e_done = s.sem("e_done")
        f_made = s.sem("f_made")
        past_made = s.sem("past_made")
        j_done = s.sem("j_done")
        tcol_made = s.sem("tcol_made")
        dst_in = s.sem("dst_in")
        src_in = s.sem("src_in")
        rel_made = s.sem("rel_made")
        srcf_made = s.sem("srcf_made")
        bf_made = s.sem("bf_made")
        turned_ = s.sem("turned")
        put = s.sem("put")
        stored = s.sem("stored")
        with nc.Block() as block:
            @block.sync
            def _(sp):
                for b in range(TB):
                    n = min(P, T - b * P)
                    sp.dma_start(last_i[0:n, b:b + 1], ins["group_last"][b * P:b * P + n, :]).then_inc(l_in, 16)
                sp.wait_ge(bf_made, 2)
                sp.dma_start(scr["rel_rows"].rearrange("(b p) e -> p b e", p=P), rel_b[:]).then_inc(stored, 16)
                sp.dma_start(scr["pen_rows"].rearrange("(b p) e -> p b e", p=P), pen_b[:]).then_inc(stored, 16)
                sp.wait_ge(stored, 32)

            @block.gpsimd
            def _(pool):
                nc.gpsimd.iota(steps_i[:], pattern=[[1, GE]], base=0, channel_multiplier=0).then_inc(iotas, 1)
                nc.gpsimd.iota(scol_i[:], pattern=[[P, SB]], base=0, channel_multiplier=1).then_inc(iotas, 1)
                pool.wait_ge(tcol_made, 1)
                for b in range(SB):
                    idx = bass.IndirectOffsetOnAxis(ap=tcol_i[:, b:b + 1], axis=0)
                    pool.indirect_dma_start(out=dst_g[:, b, :], out_offset=None, in_=ins["dst_rows"], in_offset=idx).then_inc(dst_in, 16)
                    pool.indirect_dma_start(out=src_g[:, b, :], out_offset=None, in_=ins["src_in"], in_offset=idx).then_inc(src_in, 16)

            @block.tensor
            def _(pe):
                pe.wait_ge(less_made, TB)
                for b in range(TB):
                    n = min(P, T - b * P)
                    last = nc.tensor.matmul(ps_e[:], less[0:n, b, :], ones[0:n, 0:1], start=(b == 0), stop=(b == TB - 1))
                last.then_inc(e_done, 1)
                pe.wait_ge(f_made, 1)
                nc.tensor.matmul(ps_l[:], f[:], keep["ident"][0:NT, 0:NT], start=True, stop=True)
                pe.wait_ge(past_made, 1)
                nc.tensor.matmul(ps_j[:], ones[0:NT - 1, :], past[0:NT - 1, :], start=True, stop=True)
                for b in range(SB):
                    last = nc.tensor.matmul(ps_jc[:, b:b + 1], past[0:NT - 1, b * P:(b + 1) * P], ones[0:NT - 1, 0:1], start=True, stop=True)
                last.then_inc(j_done, 1)
                for n in range(2 * SB):
                    b, src = n // 2, n % 2
                    if src:
                        pe.wait_ge(srcf_made, b + 1)
                    else:
                        pe.wait_ge(rel_made, b + 1)
                    if n >= 2:
                        pe.wait_ge(put, n - 1)
                    for t in range(TG):
                        v = srcf[:, b, t * P:(t + 1) * P] if src else rel[:, b, 1 + t * P:1 + (t + 1) * P]
                        last = nc.tensor.transpose(ps_t[n % 2][:, t, :], v, keep["ident"][:])
                    last.then_inc(turned_, 1)

            @block.vector
            def _(dve):
                n = [0]

                def link(ins_):
                    n[0] += 1
                    ins_.then_inc(step, 1)
                    dve.wait_ge(step, n[0])

                dve.wait_ge(iotas, 2)
                link(nc.vector.memset(ones[:], 1.0))
                link(nc.vector.tensor_copy(steps[:], steps_i[:]))
                link(nc.vector.tensor_copy(scol[:], scol_i[:]))
                link(nc.vector.tensor_scalar(thr[:], steps[:, 0:NT], float(P), float(P), ALU.mult, ALU.add))
                dve.wait_ge(l_in, 16 * TB)
                for b in range(TB):
                    m = min(P, T - b * P)
                    link(nc.vector.tensor_copy(last_f[0:m, b:b + 1], last_i[0:m, b:b + 1]))
                    nc.vector.tensor_scalar(less[0:m, b, :], thr[0:m, :], last_f[0:m, b:b + 1], None, ALU.is_gt).then_inc(less_made, 1)
                dve.wait_ge(e_done, 1)
                link(nc.vector.tensor_scalar(f1[:], ps_e[:], float(T - 1), 1.0, ALU.min, ALU.add))
                nc.vector.tensor_tensor(f[:], f1[:], keep["iota_p"][0:NT, :], ALU.add).then_inc(f_made, 1)
                dve.wait_ge(f_made, 1)
                nc.vector.tensor_scalar(past[:], steps[0:NT, :], f[:, 0:1], None, ALU.is_ge).then_inc(past_made, 1)
                dve.wait_ge(j_done, 1)
                nc.vector.tensor_scalar(keep["last_i"][:], ps_l[:], -1.0, None, ALU.add)
                link(nc.vector.tensor_copy(jrow[:], ps_j[:]))
                link(nc.vector.tensor_copy(jcol[:], ps_jc[:]))
                link(nc.vector.tensor_tensor(tcol[:], scol[:], jcol[:], ALU.subtract))
                nc.vector.tensor_scalar(tcol_i[:], tcol[:], float(T - 1), None, ALU.min).then_inc(tcol_made, 1)
                link(nc.vector.tensor_scalar(j128[:], jcol[:], float(P), None, ALU.mult))
                link(nc.vector.tensor_tensor(trow[:], steps[0:1, :], jrow[0:1, :], ALU.subtract))
                nc.vector.tensor_scalar(keep["t_of"][:], trow[:, 0:S], float(T - 1), None, ALU.min)
                nc.vector.tensor_copy(keep["j_of"][:], jrow[0:1, 0:S])
                nc.vector.memset(keep["same"][:, 0:1], 0.0)
                nc.vector.tensor_tensor(keep["same"][:, 1:S], jrow[:, 1:S], jrow[:, 0:S - 1], ALU.is_equal)
                dve.wait_ge(dst_in, 16 * SB)
                dve.wait_ge(src_in, 16 * SB)
                for b in range(SB):
                    link(nc.vector.tensor_scalar(rel[:, b, :], dst_g[:, b, :], j128[:, b:b + 1], None, ALU.subtract))
                    nc.vector.tensor_scalar(rel[:, b, :], rel[:, b, :], -1.0, float(P), ALU.max, ALU.min).then_inc(rel_made, 1)
                    nc.vector.tensor_copy(srcf[:, b, :], src_g[:, b, :]).then_inc(srcf_made, 1)
                dve.wait_ge(rel_made, SB)
                link(nc.vector.tensor_tensor(begin[:], rel[:, :, 1:GE + 1], rel[:, :, 0:GE], ALU.not_equal))
                nc.vector.tensor_scalar(pen_b[:], begin[:], NEG, None, ALU.mult).then_inc(bf_made, 1)
                nc.vector.tensor_copy(rel_b[:], rel[:, :, 1:GE + 1]).then_inc(bf_made, 1)
                for m in range(2 * SB):
                    b, src = m // 2, m % 2
                    dve.wait_ge(turned_, m + 1)
                    out = keep["idx_e"] if src else keep["rel_e"]
                    nc.vector.tensor_copy(out[:, b * P:(b + 1) * P, :].rearrange("p s t -> p t s"), ps_t[m % 2][:]).then_inc(put, 1)
        s.free()


def stage_scores(nc, dims, ins, keep, scr):
    S = dims["S"]
    HT = TG // 2
    with ExitStack() as st:
        s = Kit(nc, st, "s_")
        w_edge = s.sb("w_edge", [4, C])
        table = s.sb("table", [P, 2, 3, DST_W], BF16)
        feat = s.sb("feat", [4, 2, GE])
        relb = s.sb("relb", [P, 2, GE], BF16)
        hot = s.sb("hot", [P, 2, GE], BF16)
        idx = s.sb("idx", [P, 2, TG], I32)
        rows = s.sb("rows", [P, 2, TG, SRC_W])
        enc = s.sb("enc", [P, 2, HT, C])
        prod = s.sb("prod", [P, 2, HT, C])
        tmp = s.sb("tmp", [P, 2, HT, H])
        red = s.sb("red", [P, 2, HT, H])
        ps_f = [s.ps(f"ps_f{h}", [P, HT, C]) for h in range(2)]
        ps_d = [s.ps(f"ps_d{h}", [P, HT, 512]) for h in range(2)]
        w_in = s.sem("w_in")
        table_in = s.sem2("table_in")
        feat_in = s.sem2("feat_in")
        rel_in = s.sem2("rel_in")
        passed = s.sem("passed")
        rows_in = s.sem2("rows_in")
        rows_kept = s.sem2("rows_kept")
        idx_made = s.sem2("idx_made")
        hot_made = s.sem2("hot_made")
        feat_done = [s.sem2("feat_done_a"), s.sem2("feat_done_b")]
        enc_made = [s.sem2("enc_made_a"), s.sem2("enc_made_b")]
        spread = [s.sem2("spread_a"), s.sem2("spread_b")]
        multiplied = [s.sem2("multiplied_a"), s.sem2("multiplied_b")]
        tmp_made = [s.sem2("tmp_made_a"), s.sem2("tmp_made_b")]
        reduced = [s.sem2("reduced_a"), s.sem2("reduced_b")]
        scored = [s.sem2("scored_a"), s.sem2("scored_b")]

        with nc.Block() as block:
            @block.sync
            def _(sp):
                sp.dma_start(w_edge[:], ins["w_edge"]).then_inc(w_in, 16)

                def load(i, k, u):
                    t = sp.value_load(keep["t_of"][0:1, bass.ds(i, 1)], min_val=0, max_val=dims["T"] - 1)
                    j = sp.value_load(keep["j_of"][0:1, bass.ds(i, 1)], min_val=0, max_val=dims["NT"] - 1)
                    freed(sp, hot_made, k, u)
                    sp.dma_start(relb[:, u, :], row(scr["rel_rows"], i).to_broadcast([P, GE])).then_inc(rel_in[u], 16)
                    freed(sp, spread[1], k, u)
                    sp.dma_start(table[:, u].rearrange("p a w -> p (a w)"),
                                 row(scr["dst_parts"], j).rearrange("o p w -> p (o w)")).then_inc(table_in[u], 16)
                    freed(sp, feat_done[1], k, u)
                    sp.dma_start(feat[:, u, :], row(ins["edge_t"], t).rearrange("o f e -> f (o e)")).then_inc(feat_in[u], 16)

                def store(i, k, u):
                    ready(sp, rows_in, k, u, 16 * TG)
                    sp.dma_start(row(scr["rows_kept"], i).rearrange("o p w -> p (o w)"),
                                 rows[:, u].rearrange("p t w -> p (t w)")).then_inc(rows_kept[u], 16)

                skewed(sp, S, load, store)
                for u in range(2):
                    sp.wait_ge(rows_kept[u], 16 * (S // 2))

            @block.gpsimd
            def _(pool):
                def gather(i, k, u):
                    ready(pool, idx_made, k, u)
                    freed(pool, rows_kept, k, u, 16)
                    freed(pool, tmp_made[1], k, u)
                    pool.sem_inc(passed, 1)
                    for t in range(TG):
                        pool.indirect_dma_start(out=rows[:, u, t, :], out_offset=None, in_=scr["src_table"],
                                                in_offset=bass.IndirectOffsetOnAxis(ap=idx[:, u, t:t + 1], axis=0)).then_inc(rows_in[u], 16)

                pairs(pool, S, gather)

            @block.tensor
            def _(pe):
                pe.wait_ge(w_in, 16)

                def body(i, k, u):
                    for hf in range(2):
                        if hf == 0:
                            ready(pe, feat_in, k, u, 16)
                        before(pe, enc_made[hf], k, u)
                        for t in range(HT):
                            e = (hf * HT + t) * P
                            last = nc.tensor.matmul(ps_f[hf][:, t, :], feat[:, u, e:e + P], w_edge[:], start=True, stop=True)
                        last.then_inc(feat_done[hf][u], 1)
                        if hf == 0:
                            ready(pe, hot_made, k, u)
                            ready(pe, table_in, k, u, 16)
                        before(pe, tmp_made[hf], k, u)
                        for t in range(HT):
                            e = (hf * HT + t) * P
                            for part in range(3):
                                last = nc.tensor.matmul(ps_d[hf][:, t, 0:DST_W], hot[:, u, e:e + P], table[:, u, part, :],
                                                        start=(part == 0), stop=(part == 2))
                        last.then_inc(spread[hf][u], 1)

                pairs(pe, S, body)

            @block.scalar
            def _(act):
                def index(i, k, u):
                    freed(act, rows_in, k, u, 16 * TG)
                    nc.scalar.copy(idx[:, u, :], keep["idx_e"][:, bass.ds(i, 1), :].rearrange("p o t -> p (o t)")).then_inc(idx_made[u], 1)

                def encode(i, k, u):
                    for hf in range(2):
                        ready(act, feat_done[hf], k, u)
                        before(act, multiplied[hf], k, u)
                        nc.scalar.activation(enc[:, hf], ps_f[hf][:], ACT.Relu).then_inc(enc_made[hf][u], 1)

                skewed(act, S, index, encode)

            @block.vector
            def _(dve):
                def spreader(i, k, u):
                    ready(dve, rel_in, k, u, 16)
                    freed(dve, spread[1], k, u)
                    nc.vector.tensor_scalar(hot[:, u, :], relb[:, u, :], keep["iota_p"][:, 0:1], None, ALU.is_equal).then_inc(hot_made[u], 1)

                def body(i, k, u):
                    for hf in range(2):
                        ready(dve, enc_made[hf], k, u)
                        ready(dve, spread[hf], k, u)
                        before(dve, reduced[hf], k, u)
                        nc.vector.tensor_tensor(prod[:, hf], enc[:, hf], ps_d[hf][:, :, 0:C], ALU.mult).then_inc(multiplied[hf][u], 1)
                        if hf == 0:
                            ready(dve, rows_in, k, u, 16 * TG)
                        before(dve, scored[hf], k, u)
                        nc.vector.tensor_tensor(tmp[:, hf], ps_d[hf][:, :, C:DST_W], rows[:, u, hf * HT:(hf + 1) * HT, 0:H],
                                                ALU.add).then_inc(tmp_made[hf][u], 1)
                        ready(dve, multiplied[hf], k, u)
                        nc.vector.reduce_sum(red[:, hf].rearrange("p t h -> p (t h)"),
                                             prod[:, hf].rearrange("p t (h d) -> p (t h) d", d=HD), AX).then_inc(reduced[hf][u], 1)
                        ready(dve, tmp_made[hf], k, u)
                        ready(dve, reduced[hf], k, u)
                        nc.vector.tensor_tensor(keep["edge_a"][:, bass.ds(i, 1), hf * HT * H:(hf + 1) * HT * H],
                                                red[:, hf].rearrange("p t h -> p (t h)").unsqueeze(1),
                                                tmp[:, hf].rearrange("p t h -> p (t h)").unsqueeze(1), ALU.add).then_inc(scored[hf][u], 1)

                skewed(dve, S, spreader, body)
        s.free()


def stage_softmax(nc, dims, ins, keep, scr):
    S = dims["S"]
    Q = S // 4
    CH = P // H
    L = S * GE // CH
    a = keep["edge_a"][:].rearrange("p s c -> p (s c)")
    PIECE = 4
    with ExitStack() as st:
        s = Kit(nc, st, "x_")
        b_t = s.sb("b", [P, L])
        b = b_t[:]
        pen_t = s.sb("pen", [P, L + 1], BF16)
        pen = pen_t[:]
        mid = s.sb("mid", [P, 1])
        ends = s.sb("ends", [P, 2])
        chain = s.sb("chain", [H, 2, CH])
        scanned = s.sb("scanned", [H, CH])
        carry8 = s.sb("carry8", [H, CH])
        carry = s.sb("carry", [P, 1])
        ps_x = [s.ps(f"ps_x{u}", [P, 4, P]) for u in range(2)]
        pen_in = s.sem("pen_in")
        slot = s.sb("slot", [P, 2, 4 * P])
        staged = s.sem2("staged")
        staged_b = s.sem2("staged_b")
        turned_ = s.sem2("turned")
        put = s.sem2("put")
        tail_turned = s.sem("tail_turned")
        tail_put = s.sem("tail_put")
        scores_out = s.sem("scores_out")
        scores_in = s.sem("scores_in")
        step = s.sem("step")
        ends_made = s.sem("ends_made")
        ends_out = s.sem("ends_out")
        ends_in = s.sem("ends_in")
        carry_made = s.sem("carry_made")
        carry_out = s.sem("carry_out")
        carry_in = s.sem("carry_in")
        shifted = s.sem("shifted")
        exps = s.sem("exps")
        exps_out = s.sem("exps_out")
        exps_in = s.sem("exps_in")
        turned_b = s.sem2("turned_b")
        put_b = s.sem2("put_b")
        tail_turned_b = s.sem("tail_turned_b")
        tail_put_b = s.sem("tail_put_b")
        G4 = Q // 4
        REST = Q % 4
        assert G4 % 2 == 0

        def stage_in(pool, src, staged, turned):
            def body(i, k, u):
                freed(pool, turned, k, u)
                nc.gpsimd.tensor_copy(slot[:, u, :], src[:, bass.ds(i * 4 * P, 4 * P)]).then_inc(staged[u], 1)
            pairs(pool, G4, body)
            if REST:
                pool.wait_ge(turned[0], G4 // 2)
                nc.gpsimd.tensor_copy(slot[:, 0, 0:REST * P], src[:, 4 * G4 * P:Q * P]).then_inc(staged[0], 1)

        def turn(pe, staged, turned, put_, t_turned):
            def body(i, k, u):
                ready(pe, staged, k, u)
                freed(pe, put_, k, u)
                for m in range(4):
                    last = nc.tensor.transpose(ps_x[u][:, m, :], slot[:, u, m * P:(m + 1) * P], keep["ident"][:])
                last.then_inc(turned[u], 1)
            pairs(pe, G4, body)
            if REST:
                pe.wait_ge(staged[0], G4 // 2 + 1)
                pe.wait_ge(put_[0], G4 // 2)
                for m in range(REST):
                    last = nc.tensor.transpose(ps_x[0][:, m, :], slot[:, 0, m * P:(m + 1) * P], keep["ident"][:])
                last.then_inc(t_turned, 1)

        def put_all(eng, copy, u, dst, turned, put_, t_turned, t_put):
            with eng.Fori(0, G4 // 2) as k:
                eng.wait_ge(turned[u], k + 1)
                copy(dst[:, bass.ds((2 * k + u) * 512, 512)], ps_x[u][:].rearrange("p m e -> p (m e)")).then_inc(put_[u], 1)
            if u == 0 and REST:
                eng.wait_ge(t_turned, 1)
                copy(dst[:, 4 * G4 * P:Q * P], ps_x[0][:, 0:REST, :].rearrange("p m e -> p (m e)")).then_inc(t_put, 1)

        def backwards(t, n, lo=0):
            v = t[:, lo:lo + n]
            return bass.AP(v.tensor, v.offset + n - 1, [v.ap[0], [-1, n]])

        by_step = lambda d: d.rearrange("h (q s t e) -> s t h q e", s=4, t=TG, e=P)
        by_chunk = lambda d: d.rearrange("h (c l) -> c h l", c=CH)

        with nc.Block() as block:
            @block.tensor
            def _(pe):
                turn(pe, staged, turned_, put, tail_turned)
                turn(pe, staged_b, turned_b, put_b, tail_turned_b)

            @block.gpsimd
            def _(pool):
                stage_in(pool, a, staged, turned_)
                pool.wait_ge(exps_in, 16 * CH)
                if REST:
                    pool.wait_ge(tail_turned, 1)
                stage_in(pool, b, staged_b, turned_b)

            @block.sync
            def _(sp):
                for c in range(CH):
                    v = scr["pen_rows"].rearrange("s e -> (s e)")[c * L:(c + 1) * L + 1]
                    sp.dma_start(pen[c * H:(c + 1) * H, :], v.partition_broadcast(H)).then_inc(pen_in, 16)
                for u in range(2):
                    sp.wait_ge(put[u], G4 // 2)
                if REST:
                    sp.wait_ge(tail_put, 1)
                for m in range(CH):
                    sp.dma_start(by_step(scr["score_t"])[m // TG, m % TG],
                                 b[m * H:(m + 1) * H, :].rearrange("p (q e) -> p q e", e=P)).then_inc(scores_out, 16)
                sp.wait_ge(scores_out, 16 * CH)
                for c in range(CH):
                    sp.dma_start(a[c * H:(c + 1) * H, :], by_chunk(scr["score_t"])[c]).then_inc(scores_in, 16)
                for n in range(2):
                    sp.wait_ge(ends_made, n + 1)
                    sp.dma_start(scr["ends"], ends[:]).then_inc(ends_out, 16)
                    sp.wait_ge(ends_out, 16 * (n + 1))
                    for w in range(2):
                        sp.dma_start(chain[:, w, :], scr["ends"].rearrange("(c h) w -> w h c", h=H)[w],
                                     allow_slow_non_contiguous=True).then_inc(ends_in, 16)
                    sp.wait_ge(carry_made, n + 1)
                    sp.dma_start(scr["carry"], carry8[:]).then_inc(carry_out, 16)
                    sp.wait_ge(carry_out, 16 * (n + 1))
                    for c in range(CH):
                        sp.dma_start(carry[c * H:(c + 1) * H, :], scr["carry"][:, c:c + 1],
                                     allow_slow_non_contiguous=True).then_inc(carry_in, 16)
                sp.wait_ge(exps, PIECE)
                for c in range(CH):
                    sp.dma_start(by_chunk(scr["exp_t"])[c], a[c * H:(c + 1) * H, :]).then_inc(exps_out, 16)
                sp.wait_ge(exps_out, 16 * CH)
                for m in range(CH):
                    sp.dma_start(b[m * H:(m + 1) * H, :].rearrange("p (q e) -> p q e", e=P),
                                 by_step(scr["exp_t"])[m // TG, m % TG]).then_inc(exps_in, 16)

            @block.scalar
            def _(act):
                put_all(act, nc.scalar.copy, 0, b, turned_, put, tail_turned, tail_put)
                for m in range(PIECE):
                    act.wait_ge(shifted, m + 1)
                    cut = slice(m * L // PIECE, (m + 1) * L // PIECE)
                    nc.scalar.activation(a[:, cut], a[:, cut], ACT.Exp).then_inc(exps, 1)
                put_all(act, nc.scalar.copy, 0, a, turned_b, put_b, tail_turned_b, tail_put_b)

            @block.vector
            def _(dve):
                n = [0]

                def link(ins_):
                    n[0] += 1
                    ins_.then_inc(step, 1)
                    dve.wait_ge(step, n[0])

                put_all(dve, nc.vector.tensor_copy, 1, b, turned_, put, tail_turned, tail_put)
                dve.wait_ge(pen_in, 16 * CH)
                link(nc.vector.tensor_reduce(mid[:], pen[:, 1:L], AX, ALU.min))
                dve.wait_ge(scores_in, 16 * CH)
                link(nc.vector.scalar_tensor_tensor(out=a, in0=a, scalar=SLOPE, in1=a, op0=ALU.mult, op1=ALU.max))

                def chunks(n_, edge_cut, value):
                    link(nc.vector.tensor_tensor(ends[:, 1:2], mid[:], edge_cut, ALU.min))
                    nc.vector.tensor_copy(ends[:, 0:1], value).then_inc(ends_made, 1)
                    dve.wait_ge(ends_in, 32 * (n_ + 1))
                    rev = n_ == 1
                    va, cu, out = chain[:, 0, :], chain[:, 1, :], scanned[:]
                    if rev:
                        va, cu, out = backwards(va, CH), backwards(cu, CH), backwards(out, CH)
                    link(nc.vector.tensor_tensor_scan(out, cu, va, NEG, ALU.add, ALU.max))
                    if rev:
                        link(nc.vector.memset(carry8[:, CH - 1:CH], NEG))
                        nc.vector.tensor_copy(carry8[:, 0:CH - 1], scanned[:, 1:CH]).then_inc(carry_made, 1)
                    else:
                        link(nc.vector.memset(carry8[:, 0:1], NEG))
                        nc.vector.tensor_copy(carry8[:, 1:CH], scanned[:, 0:CH - 1]).then_inc(carry_made, 1)
                    dve.wait_ge(carry_in, 16 * CH * (n_ + 1))

                link(nc.vector.tensor_tensor_scan(b, pen[:, 0:L], a, NEG, ALU.add, ALU.max))
                chunks(0, pen[:, 0:1], b[:, L - 1:L])
                link(nc.vector.tensor_tensor_scan(b, pen[:, 0:L], a, carry[:, 0:1], ALU.add, ALU.max))
                cut_b, b_rev = backwards(pen, L, 1), backwards(b, L)
                link(nc.vector.tensor_tensor_scan(b_rev, cut_b, b_rev, NEG, ALU.add, ALU.max))
                chunks(1, pen[:, L:L + 1], b[:, 0:1])
                link(nc.vector.tensor_tensor_scan(b_rev, cut_b, b_rev, carry[:, 0:1], ALU.add, ALU.max))
                for m in range(PIECE):
                    cut = slice(m * L // PIECE, (m + 1) * L // PIECE)
                    nc.vector.tensor_tensor(a[:, cut], a[:, cut], b[:, cut], ALU.subtract).then_inc(shifted, 1)
                put_all(dve, nc.vector.tensor_copy, 1, a, turned_b, put_b, tail_turned_b, tail_put_b)
        s.free()


def stage_aggregate(nc, dims, ins, keep, scr):
    S = dims["S"]
    with ExitStack() as st:
        s = Kit(nc, st, "g_")
        rows = s.sb("rows", [P, 2, TG, SRC_W])
        hot = s.sb("hot", [P, 2, TG, P])
        acc = s.sb("acc", [P, 2, SRC_W])
        ps_a = [s.ps(f"ps_a{u}", [P, SRC_W]) for u in range(2)]
        rows_in = s.sem2("rows_in")
        hot_made = s.sem2("hot_made")
        weighted = s.sem2("weighted")
        exps_put = s.sem2("exps_put")
        summed = s.sem2("summed")
        added = s.sem2("added")
        acc_stored = s.sem2("acc_stored")
        cleared = s.sem("cleared")
        with nc.Block() as block:
            @block.sync
            def _(sp):
                def load(i, k, u):
                    freed(sp, summed, k, u)
                    sp.dma_start(rows[:, u].rearrange("p t w -> p (t w)"),
                                 row(scr["rows_kept"], i).rearrange("o p w -> p (o w)")).then_inc(rows_in[u], 16)

                def store(i, k, u):
                    ready(sp, added, k, u)
                    sp.dma_start(row(scr["sums"], i).rearrange("o p w -> p (o w)"), acc[:, u, :]).then_inc(acc_stored[u], 16)

                skewed(sp, S, load, store)
                for u in range(2):
                    sp.wait_ge(acc_stored[u], 16 * (S // 2))

            @block.scalar
            def _(act):
                def body(i, k, u):
                    ready(act, rows_in, k, u, 16)
                    nc.scalar.copy(rows[:, u, :, 0:H], keep["edge_a"][:, bass.ds(i, 1), :].rearrange("p o (t h) -> p (o t) h", t=TG)).then_inc(exps_put[u], 1)

                pairs(act, S, body)

            @block.tensor
            def _(pe):
                def body(i, k, u):
                    ready(pe, hot_made, k, u)
                    ready(pe, weighted, k, u)
                    ready(pe, exps_put, k, u)
                    freed(pe, added, k, u)
                    for t in range(TG):
                        last = nc.tensor.matmul(ps_a[u][:], hot[:, u, t, :], rows[:, u, t, :], start=(t == 0), stop=(t == TG - 1))
                    last.then_inc(summed[u], 1)

                pairs(pe, S, body)

            @block.vector
            def _(dve):
                nc.vector.memset(acc[:], 0.0).then_inc(cleared, 1)
                dve.wait_ge(cleared, 1)

                def weigh(i, k, u):
                    freed(dve, summed, k, u)
                    nc.vector.tensor_tensor(hot[:, u], keep["rel_e"][:, bass.ds(i, 1), :].rearrange("p o t -> p (o t)").unsqueeze(2).to_broadcast([P, TG, P]),
                                            keep["iota_row"][:].unsqueeze(1).to_broadcast([P, TG, P]), ALU.is_equal).then_inc(hot_made[u], 1)
                    ready(dve, rows_in, k, u, 16)
                    v = rows[:, u, :, H:SRC_W].rearrange("p t (h d) -> p t h d", d=HD)
                    nc.vector.tensor_tensor(v, v, keep["edge_a"][:, bass.ds(i, 1), :].rearrange("p o (t h) -> p (o t) h", t=TG).unsqueeze(3).to_broadcast([P, TG, H, HD]),
                                            ALU.mult).then_inc(weighted[u], 1)

                def add(i, k, u):
                    ready(dve, summed, k, u)
                    before(dve, added, k, u)
                    freed(dve, acc_stored, k, u, 16)
                    nc.vector.scalar_tensor_tensor(out=acc[:, u, :], in0=acc[:, 1 - u, :], scalar=keep["same"][:, bass.ds(i, 1)],
                                                   in1=ps_a[u][:], op0=ALU.mult, op1=ALU.add).then_inc(added[u], 1)

                skewed(dve, S, weigh, add)
        s.free()



def stage_combine(nc, dims, ins, keep, scr):
    NT = dims["NT"]
    with ExitStack() as st:
        s = Kit(nc, st, "b_")
        wr = s.sb("wr", [P, 2, EXPERTS])
        br = s.sb("br", [P, EXPERTS])
        bo = s.sb("bo", [EXPERTS, C])
        sums = s.sb("sums", [P, 2, SRC_W])
        xm = s.sb("xm", [P, 2, C])
        x1 = s.sb("x1", [P, 2, C])
        y = s.sb("y", [P, 2, C])
        den = s.sb("den", [P, 2, H])
        rden = s.sb("rden", [P, 2, H])
        stats = s.sb("stats", [P, 2, 6])
        mv = s.sb("mv", [P, 2, 2])
        std = s.sb("std", [P, 2, 1])
        veps = s.sb("veps", [P, 2, 1])
        rstd = s.sb("rstd", [P, 2, 1])
        lg = s.sb("lg", [P, 2, EXPERTS])
        mx = s.sb("mx", [P, 2, 1])
        ex = s.sb("ex", [P, 2, EXPERTS])
        tot = s.sb("tot", [P, 2, 1])
        rtot = s.sb("rtot", [P, 2, 1])
        gate = s.sb("gate", [P, 2, EXPERTS])
        xT = s.sb("xT", [P, 2, 2, P])
        gateT = s.sb("gateT", [EXPERTS, 2, P])
        ps_t = [s.ps(f"ps_t{u}", [P, 2, P]) for u in range(2)]
        ps_l = s.ps("ps_l", [P, EXPERTS])
        ps_g = s.ps("ps_g", [P, P])
        ps_b = s.ps("ps_b", [P, C])
        w_in = s.sem("w_in")
        passed = s.sem("passed")
        names = ("sums_in xm_in den_made rden_made y_made x1_made stats_made mv_made veps_made std_made rstd_made ln_made "
                 "turned xT_made logits_done lg_made mx_made shifted ex_made tot_made rtot_made gate_made gate_turned gateT_made "
                 "bias_done start_made xT_kept").split()
        m = {n: s.sem2(n) for n in names}
        with nc.Block() as block:
            @block.sync
            def _(sp):
                sp.dma_start(wr[:], ins["Wr"]).then_inc(w_in, 16)
                sp.dma_start(br[:], ins["br"].partition_broadcast(P)).then_inc(w_in, 16)
                sp.dma_start(bo[:], ins["bo"]).then_inc(w_in, 16)

                def body(i, k, u):
                    last = sp.value_load(keep["last_i"][0:1, bass.ds(i, 1)], min_val=0, max_val=dims["S"] - 1)
                    freed(sp, m["y_made"], k, u)
                    sp.dma_start(sums[:, u, :], row(scr["sums"], last).rearrange("o p w -> p (o w)")).then_inc(m["sums_in"][u], 16)
                    freed(sp, m["x1_made"], k, u)
                    sp.dma_start(xm[:, u, :], row(scr["x_mix"], i).rearrange("o p w -> p (o w)")).then_inc(m["xm_in"][u], 16)

                pairs(sp, NT, body)

            @block.vector
            def _(dve):
                dve.wait_ge(w_in, 48)

                def body(i, k, u):
                    V = nc.vector
                    ready(dve, m["sums_in"], k, u, 16)
                    V.tensor_scalar(den[:, u], sums[:, u, 0:H], DEN_MIN, None, ALU.max).then_inc(m["den_made"][u], 1)
                    ready(dve, m["den_made"], k, u)
                    V.reciprocal(rden[:, u], den[:, u]).then_inc(m["rden_made"][u], 1)
                    ready(dve, m["rden_made"], k, u)
                    V.tensor_tensor(y[:, u, :].rearrange("p (h d) -> p h d", h=H), sums[:, u, H:SRC_W].rearrange("p (h d) -> p h d", h=H),
                                    rden[:, u].unsqueeze(2).to_broadcast([P, H, HD]), ALU.mult).then_inc(m["y_made"][u], 1)
                    ready(dve, m["y_made"], k, u)
                    ready(dve, m["xm_in"], k, u, 16)
                    freed(dve, m["start_made"], k, u)
                    V.tensor_tensor(x1[:, u, :], y[:, u, :], xm[:, u, :], ALU.add).then_inc(m["x1_made"][u], 1)
                    ready(dve, m["x1_made"], k, u)
                    V.bn_stats(stats[:, u, :], x1[:, u, :]).then_inc(m["stats_made"][u], 1)
                    ready(dve, m["stats_made"], k, u)
                    dve.sem_inc(passed, 1)
                    V.bn_aggr(mv[:, u, :], stats[:, u, :]).then_inc(m["mv_made"][u], 1)
                    ready(dve, m["mv_made"], k, u)
                    V.tensor_scalar(veps[:, u], mv[:, u, 1:2], LN_EPS, None, ALU.add).then_inc(m["veps_made"][u], 1)
                    ready(dve, m["std_made"], k, u)
                    V.reciprocal(rstd[:, u], std[:, u]).then_inc(m["rstd_made"][u], 1)
                    ready(dve, m["rstd_made"], k, u)
                    freed(dve, m["turned"], k, u)
                    V.tensor_scalar(y[:, u, :], x1[:, u, :], mv[:, u, 0:1], rstd[:, u], ALU.subtract, ALU.mult).then_inc(m["ln_made"][u], 1)
                    ready(dve, m["logits_done"], k, u)
                    V.tensor_tensor(lg[:, u], ps_l[:], br[:], ALU.add).then_inc(m["lg_made"][u], 1)
                    ready(dve, m["lg_made"], k, u)
                    V.reduce_max(mx[:, u], lg[:, u], AX).then_inc(m["mx_made"][u], 1)
                    ready(dve, m["mx_made"], k, u)
                    V.tensor_scalar(lg[:, u], lg[:, u], mx[:, u], None, ALU.subtract).then_inc(m["shifted"][u], 1)
                    ready(dve, m["ex_made"], k, u)
                    V.reduce_sum(tot[:, u], ex[:, u], AX).then_inc(m["tot_made"][u], 1)
                    ready(dve, m["tot_made"], k, u)
                    V.reciprocal(rtot[:, u], tot[:, u]).then_inc(m["rtot_made"][u], 1)
                    ready(dve, m["rtot_made"], k, u)
                    freed(dve, m["gate_turned"], k, u)
                    V.tensor_scalar(keep["gate"][:, bass.ds(i, 1), :].rearrange("p o e -> p (o e)"), ex[:, u], rtot[:, u], None, ALU.mult)
                    V.tensor_scalar(gate[:, u], ex[:, u], rtot[:, u], None, ALU.mult).then_inc(m["gate_made"][u], 1)
                    ready(dve, m["bias_done"], k, u)
                    V.tensor_tensor(keep["y_all"][:, bass.ds(i, 1), :], ps_b[:].unsqueeze(1), x1[:, u, :].unsqueeze(1), ALU.add).then_inc(m["start_made"][u], 1)

                pairs(dve, NT, body)

            @block.gpsimd
            def _(pool):
                def body(i, k, u):
                    ready(pool, m["xT_made"], k, u)
                    nc.gpsimd.tensor_copy(keep["xT"][:, :, bass.ds(i * P, P)], xT[:, u]).then_inc(m["xT_kept"][u], 1)

                pairs(pool, NT, body)

            @block.scalar
            def _(act):
                def body(i, k, u):
                    ready(act, m["veps_made"], k, u)
                    nc.scalar.activation(std[:, u], veps[:, u], ACT.Sqrt).then_inc(m["std_made"][u], 1)
                    ready(act, m["turned"], k, u)
                    freed(act, m["logits_done"], k, u)
                    freed(act, m["xT_kept"], k, u)
                    nc.scalar.copy(xT[:, u], ps_t[u][:]).then_inc(m["xT_made"][u], 1)
                    ready(act, m["shifted"], k, u)
                    nc.scalar.activation(ex[:, u], lg[:, u], ACT.Exp).then_inc(m["ex_made"][u], 1)
                    ready(act, m["gate_turned"], k, u)
                    nc.scalar.copy(gateT[:, u, :], ps_g[0:EXPERTS, :]).then_inc(m["gateT_made"][u], 1)

                pairs(act, NT, body)

            @block.tensor
            def _(pe):
                pe.wait_ge(w_in, 48)

                def body(i, k, u):
                    ready(pe, m["ln_made"], k, u)
                    for c in range(2):
                        last = nc.tensor.transpose(ps_t[u][:, c, :], y[:, u, c * P:(c + 1) * P], keep["ident"][:])
                    last.then_inc(m["turned"][u], 1)
                    ready(pe, m["xT_made"], k, u)
                    before(pe, m["lg_made"], k, u)
                    for c in range(2):
                        last = nc.tensor.matmul(ps_l[:], xT[:, u, c, :], wr[:, c, :], start=(c == 0), stop=(c == 1))
                    last.then_inc(m["logits_done"][u], 1)
                    ready(pe, m["gate_made"], k, u)
                    before(pe, m["gateT_made"], k, u)
                    nc.tensor.matmul(ps_g[0:EXPERTS, :], gate[:, u], keep["ident"][:], start=True, stop=True).then_inc(m["gate_turned"][u], 1)
                    ready(pe, m["gateT_made"], k, u)
                    before(pe, m["start_made"], k, u)
                    nc.tensor.matmul(ps_b[:], gateT[:, u, :], bo[:], start=True, stop=True).then_inc(m["bias_done"][u], 1)

                pairs(pe, NT, body)
        s.free()


def stage_experts(nc, dims, ins, keep, scr, out):
    NT = dims["NT"]
    SB = 7
    NS = NT // SB
    W = SB * P // 2
    with ExitStack() as st:
        s = Kit(nc, st, "e_")
        w = {n: s.sb(n, [P, EXPERTS, 2, C]) for n in ("W1", "W2", "Wo")}
        norm = {n: s.sb(n, [P, EXPERTS, 2]) for n in ("b1", "g1", "be1", "m1", "v1", "b2", "g2", "be2", "m2", "v2")}
        scale = {n: s.sb(f"scale{n}", [P, EXPERTS, 2]) for n in "12"}
        shift = {n: s.sb(f"shift{n}", [P, EXPERTS, 2]) for n in "12"}
        h1 = s.sb("h1", [P, 2, 2 * W])
        h2 = s.sb("h2", [P, 2, 2 * W])
        ps = [s.ps(f"ps{b}", [P, 512]) for b in range(4)]
        ps_o = [s.ps(f"ps_o{b}", [P, 2, C]) for b in range(4)]
        norm_in = s.sem("norm_in")
        w_in = [s.sem(f"w_in{e}") for e in range(EXPERTS)]
        step = s.sem("step")
        veps_made = s.sem("veps_made")
        std_made = s.sem("std_made")
        norm_made = s.sem("norm_made")
        l1_done = [s.sem(f"l1_done{q}") for q in range(4)]
        h1_made = [s.sem(f"h1_made{q}") for q in range(4)]
        l2_done = [s.sem(f"l2_done{q}") for q in range(4)]
        h2_made = [s.sem(f"h2_made{q}") for q in range(4)]
        o_done = [s.sem(f"o_done{b}") for b in range(4)]
        o_added = [s.sem(f"o_added{b}") for b in range(4)]
        out_stored = s.sem("out_stored")

        with nc.Block() as block:
            @block.sync
            def _(sp):
                for n in norm:
                    sp.dma_start(norm[n][:], ins[n]).then_inc(norm_in, 16)
                for e in range(EXPERTS):
                    for n in w:
                        sp.dma_start(w[n][:, e], ins[n][:, e]).then_inc(w_in[e], 16)
                def body(i):
                    sp.wait_ge(o_added[3], EXPERTS * (i + 1))
                    sp.dma_start(out[:, bass.ds(i * SB, SB), :], keep["y_all"][:, bass.ds(i * SB, SB), :]).then_inc(out_stored, 16)

                turns(sp, NS, body)
                sp.wait_ge(out_stored, 16 * NS)

            @block.vector
            def _(dve):
                n = [0]

                def link(ins_):
                    n[0] += 1
                    ins_.then_inc(step, 1)
                    dve.wait_ge(step, n[0])

                dve.wait_ge(norm_in, 160)
                V = nc.vector
                for q in "12":
                    V.tensor_scalar(norm["v" + q][:], norm["v" + q][:], BN_EPS, None, ALU.add).then_inc(veps_made, 1)
                for m, q in enumerate("12"):
                    dve.wait_ge(std_made, m + 1)
                    link(V.reciprocal(norm["v" + q][:], norm["v" + q][:]))
                    link(V.tensor_tensor(scale[q][:], norm["g" + q][:], norm["v" + q][:], ALU.mult))
                    link(V.tensor_tensor(shift[q][:], norm["b" + q][:], norm["m" + q][:], ALU.subtract))
                    link(V.tensor_tensor(shift[q][:], shift[q][:], scale[q][:], ALU.mult))
                    V.tensor_tensor(shift[q][:], shift[q][:], norm["be" + q][:], ALU.add).then_inc(norm_made, 1)
                def body(i):
                    for e in range(EXPERTS):
                        turn = i * EXPERTS + e
                        for b in range(SB):
                            q, r = b // 2, b % 2
                            if r == 0:
                                dve.wait_ge(o_done[q], turn + 1)
                            pq = 2 if q < 3 else 1
                            wait(dve, o_added[q], turn * pq)
                            y = keep["y_all"][:, bass.ds(i * SB + b, 1), :].rearrange("p o c -> p (o c)")
                            V.scalar_tensor_tensor(out=y, in0=ps_o[q][:, r, :], scalar=keep["gate"][:, bass.ds(i * SB + b, 1), e:e + 1].rearrange("p o e -> p (o e)"),
                                                   in1=y, op0=ALU.mult, op1=ALU.add).then_inc(o_added[q], 1)

                turns(dve, NS, body)

            @block.scalar
            def _(act):
                for m, q in enumerate("12"):
                    act.wait_ge(veps_made, m + 1)
                    nc.scalar.activation(norm["v" + q][:], norm["v" + q][:], ACT.Sqrt).then_inc(std_made, 1)
                act.wait_ge(norm_made, 2)

                def body(i):
                    for e in range(EXPERTS):
                        turn = i * EXPERTS + e
                        for q in range(4):
                            m, hf = q // 2, q % 2
                            act.wait_ge(l1_done[q], turn + 1)
                            wait(act, l2_done[3], turn)
                            nc.scalar.activation(h1[:, m, hf * W:(hf + 1) * W], ps[q][:, 0:W], ACT.Relu,
                                                 scale=scale["1"][:, e, m:m + 1], bias=shift["1"][:, e, m:m + 1]).then_inc(h1_made[q], 1)
                        for q in range(4):
                            m, hf = q // 2, q % 2
                            act.wait_ge(l2_done[q], turn + 1)
                            wait(act, o_done[3], turn)
                            nc.scalar.activation(h2[:, m, hf * W:(hf + 1) * W], ps[q][:, 0:W], ACT.Relu,
                                                 scale=scale["2"][:, e, m:m + 1], bias=shift["2"][:, e, m:m + 1]).then_inc(h2_made[q], 1)

                turns(act, NS, body)

            @block.tensor
            def _(pe):
                def body(i):
                    for e in range(EXPERTS):
                        turn = i * EXPERTS + e
                        pe.wait_ge(w_in[e], 48)
                        for q in range(4):
                            m, hf = q // 2, q % 2
                            wait(pe, h2_made[q], turn)
                            for c in range(2):
                                last = nc.tensor.matmul(ps[q][:, 0:W], w["W1"][:, e, c, m * P:(m + 1) * P],
                                                        keep["xT"][:, c, bass.ds(i * 2 * W + hf * W, W)],
                                                        start=(c == 0), stop=(c == 1))
                            last.then_inc(l1_done[q], 1)
                        for q in range(4):
                            m, hf = q // 2, q % 2
                            pe.wait_ge(h1_made[hf], turn + 1)
                            pe.wait_ge(h1_made[2 + hf], turn + 1)
                            pe.wait_ge(h1_made[q], turn + 1)
                            for c in range(2):
                                last = nc.tensor.matmul(ps[q][:, 0:W], w["W2"][:, e, c, m * P:(m + 1) * P],
                                                        h1[:, c, hf * W:(hf + 1) * W], start=(c == 0), stop=(c == 1))
                            last.then_inc(l2_done[q], 1)
                        for b in range(SB):
                            q, r = b // 2, b % 2
                            if b in (0, SB // 2):
                                for m in range(2):
                                    pe.wait_ge(h2_made[2 * m + (b > 0)], turn + 1)
                            if r == 0:
                                wait(pe, o_added[q], turn * (2 if q < 3 else 1))
                            for c in range(2):
                                last = nc.tensor.matmul(ps_o[q][:, r, :], h2[:, c, b * P:(b + 1) * P], w["Wo"][:, e, c, :],
                                                        start=(c == 0), stop=(c == 1))
                            if r == 1 or b == SB - 1:
                                last.then_inc(o_done[q], 1)

                turns(pe, NS, body)
        s.free()


def build(nc, dims, ins, out):
    NT, S = dims["NT"], dims["S"]

    def dram(name, shape, dt=F32):
        return nc.dram_tensor("scratch_" + name, shape, dt, kind="Internal").ap()

    scr = dict(
        src_rows=dram("src_rows", (NT, P, SRC_W)), dst_parts=dram("dst_parts", (NT, P, 3 * DST_W), BF16),
        q_rows=dram("q_rows", (NT, P, H * EXT)), x_mix=dram("x_mix", (NT, P, C)),
        rel_rows=dram("rel_rows", (512, GE), BF16), pen_rows=dram("pen_rows", (512, GE), BF16),
        rows_kept=dram("rows_kept", (S, P, TG * SRC_W)), score_t=dram("score_t", (H, S * GE)),
        exp_t=dram("exp_t", (H, S * GE)), ends=dram("ends", (P, 2)), carry=dram("carry", (H, P // H)),
        sums=dram("sums", (S, P, SRC_W)))
    scr["src_table"] = scr["src_rows"].rearrange("t p w -> (t p) w")

    with ExitStack() as whole:
        kit = Kit(nc, whole, "k_")
        keep = dict(ident=kit.sb("ident", [P, P]), iota_row=kit.sb("iota_row", [P, P]), iota_p=kit.sb("iota_p", [P, 1]),
                    last_i=kit.sb("last_i", [1, NT], I32))
        with ExitStack() as part:
            kit = Kit(nc, part, "kn_")
            keep.update(
                x_all=kit.sb("x_all", [P, NT, C]), w_h=kit.sb("w_h", [P, 2, ALL_W]), w_qkv=kit.sb("w_qkv", [P, 2, 3 * C]),
                b_qkv=kit.sb("b_qkv", [P, 3 * C]), w_proj=kit.sb("w_proj", [P, 2, C]), b_res=kit.sb("b_res", [P, 2, C]),
                c_out=kit.sb("c_out", [P, 2 * H]), c_in=kit.sb("c_in", [P, 2 * H]), in_range=kit.sb("in_range", [P, 1]),
                c_pair=kit.sb("c_pair", [P, 1]), rstd=kit.sb("rstd", [P, NT]), nmr=kit.sb("nmr", [P, NT]),
                g_sum=kit.sb("g_sum", [P, H * PB, VE]))
            stage_constants(nc, None, dims, ins, keep)
            stage_nodes(nc, None, dims, ins, keep, scr)
            stage_mix(nc, None, dims, ins, keep, scr)
        with ExitStack() as part:
            kit = Kit(nc, part, "ke_")
            keep.update(
                t_of=kit.sb("t_of", [1, S], I32), j_of=kit.sb("j_of", [1, S], I32), same=kit.sb("same", [P, 512]),
                idx_e=kit.sb("idx_e", [P, 512, TG], I32), rel_e=kit.sb("rel_e", [P, 512, TG]))
            stage_plan(nc, dims, ins, keep, scr)
            keep["edge_a"] = kit.sb("edge_a", [P, S, TG * H])
            stage_scores(nc, dims, ins, keep, scr)
            stage_softmax(nc, dims, ins, keep, scr)
            stage_aggregate(nc, dims, ins, keep, scr)
        with ExitStack() as part:
            kit = Kit(nc, part, "kx_")
            keep.update(xT=kit.sb("xT", [P, 2, NT * P]), y_all=kit.sb("y_all", [P, NT, C]), gate=kit.sb("gate", [P, NT, EXPERTS]))
            stage_combine(nc, dims, ins, keep, scr)
            stage_experts(nc, dims, ins, keep, scr, out)


def kernel(**inputs):
    import numpy as np
    import concourse.bacc as bacc
    from concourse.bass_utils import run_bass_kernel_spmd

    arrays, dims = lay_out(inputs)
    nc = bacc.Bacc("TRN2", target_bir_lowering=False, num_devices=1)
    ins = {n: nc.dram_tensor("in_" + n, a.shape, mybir.dt.from_np(a.dtype), kind="ExternalInput").ap() for n, a in arrays.items()}
    out = nc.dram_tensor("out_rows", (dims["NT"] * P, C), F32, kind="ExternalOutput").ap()
    build(nc, dims, ins, out.rearrange("(t p) c -> p t c", p=P))
    r = run_bass_kernel_spmd(nc, [{"in_" + n: np.ascontiguousarray(a) for n, a in arrays.items()}], core_ids=[0])
    return r.results[0]["out_rows"][:dims["N"]]
```

```python
import numpy as np
import concourse.bass as bass
import concourse.mybir as mybir
from contextlib import ExitStack

F32 = mybir.dt.float32
BF16 = mybir.dt.bfloat16
I32 = mybir.dt.int32
ALU = mybir.AluOpType
ACT = mybir.ActivationFunctionType
AX = mybir.AxisListType.X

P = 128
C = 256
H = 8
HD = C // H
EXPERTS = 8
LN_EPS = 1e-5
NORM_EPS = 1e-12
BN_EPS = 1e-3
DEN_MIN = 1e-10
SLOPE = 0.2
QK_SCALE = float(HD) ** 0.25

AUG = HD + 1
TURNS = AUG // 2 + 1
EXT = AUG + TURNS - 1
PAIRS = TURNS * AUG
PB = -(-PAIRS // P)
VE = HD + 1
POOL_HEADS = 2
SRC_W = H + C
PRODUCTS = ((0, 0), (0, 1), (0, 2), (1, 0), (1, 1), (2, 0), (1, 2), (2, 1))
EF = 3
DST_W = C + H
ALL_W = H + C + H
TG = 4
GE = TG * P
NEG = -3.0e38


def wait(eng, sem, value):
    if not (isinstance(value, int) and value <= 0):
        eng.wait_ge(sem, value)


def ready(eng, sem, k, u, inc=1):
    wait(eng, sem[u], inc * (k + 1))


def freed(eng, sem, k, u, inc=1):
    wait(eng, sem[u], inc * k)


def before(eng, sem, k, u, inc=1):
    wait(eng, sem[u - 1], inc * (k + (u > 0)))


def turns(eng, n, body):
    body(0)
    if n > 1:
        with eng.Fori(1, n) as k:
            body(k)


def pairs(eng, n, body):
    def two(k):
        body(2 * k, k, 0)
        body(2 * k + 1, k, 1)

    if n > 1:
        turns(eng, n // 2, two)
    if n % 2:
        body(n - 1, n // 2, 0)


def skewed(eng, n, ahead, body):
    def two(k):
        ahead(2 * k + 1, k, 1)
        body(2 * k, k, 0)
        ahead(2 * k + 2, k + 1, 0)
        body(2 * k + 1, k, 1)

    ahead(0, 0, 0)
    half = (n - 1) // 2
    turns(eng, half, two)
    if n % 2 == 0:
        ahead(n - 1, half, 1)
        body(n - 2, half, 0)
        body(n - 1, half, 1)
    else:
        body(n - 1, half, 0)


def woven(eng, n, step):
    def two(k):
        step((2 * k + 1, k, 1), (2 * k, k, 0))
        step((2 * k + 2, k + 1, 0), (2 * k + 1, k, 1))

    step((0, 0, 0), None)
    turns(eng, n // 2, two)
    step(None, (n - 1, n // 2, 0))


def led(eng, n, first, ahead, last):
    def one(i, k, u, more=True):
        first(i, k, u)
        if more:
            ahead(i + 2, k + 1, u)
        last(i, k, u)

    def two(k):
        one(2 * k, k, 0)
        one(2 * k + 1, k, 1)

    ahead(0, 0, 0)
    ahead(1, 0, 1)
    turns(eng, (n - 3) // 2, two)
    k = n // 2
    one(n - 3, k - 1, 0)
    one(n - 2, k - 1, 1, False)
    one(n - 1, k, 0, False)


def none(i, k, u):
    pass


def staggered(eng, n, ring, lead, ahead, body):
    def turn(k, end=ring):
        for u in range(ring):
            if u + lead < end:
                ahead(k * ring + u + lead, k + (u + lead) // ring, (u + lead) % ring)
            body(k * ring + u, k, u)

    for m in range(lead):
        ahead(m, 0, m)
    turn(0, 2 * ring)
    with eng.Fori(1, n // ring - 1) as k:
        turn(k, 2 * ring)
    turn(n // ring - 1)


class Kit:

    def __init__(self, nc, stack, tag=""):
        self.nc, self.stack, self.tag, self.sems = nc, stack, tag, []

    def sb(self, name, shape, dt=F32):
        return self.stack.enter_context(self.nc.sbuf_tensor(self.tag + name, shape, dt))

    def ps(self, name, shape, dt=F32):
        return self.stack.enter_context(self.nc.psum_tensor(self.tag + name, shape, dt))

    def sem(self, name):
        self.sems.append(self.nc.alloc_semaphore(self.tag + name))
        return self.sems[-1]

    def free(self):
        self.nc.clear_and_free_semaphores(self.sems)
        self.nc.all_engine_barrier()

    def sem2(self, name, slots=2):
        return [self.sem(f"{name}_{u}") for u in range(slots)]


def row(d, i):
    return d[bass.ds(i, 1)]


def stage_constants(nc, g, dims, ins, keep):
    NT, N = dims["NT"], dims["N"]
    with ExitStack() as st:
        s = Kit(nc, st, "c_")
        w_nat = s.sb("w_nat", [P, 2, C])
        a_blk = s.sb("a_blk", [P, 2, 2 * H])
        stats = s.sb("stats", [P, NT, 6])
        t0 = s.sb("t0", [P, NT])
        t1 = s.sb("t1", [P, NT])
        mean = s.sb("mean", [P, NT])
        var = s.sb("var", [P, NT])
        ones = s.sb("ones", [P, P])
        iota_i = s.sb("iota_i", [P, P], I32)
        iota_pi = s.sb("iota_pi", [P, 1], I32)
        ps_fold = s.ps("ps_fold", [P, 2, 2 * H])
        NX = 7
        XB = NT // NX
        x_in = [s.sem(f"x_in{b}") for b in range(NX)]
        w_in = s.sem("w_in")
        ones_set = s.sem("ones_set")
        consts_made = s.sem("consts_made")
        folded = s.sem("folded")
        fold_put = s.sem("fold_put")
        stats_made = s.sem("stats_made")
        step = s.sem("step")
        var_made = s.sem("var_made")
        std_made = s.sem("std_made")
        with nc.Block() as block:
            @block.sync
            def _(sp):
                sp.dma_start(w_nat[:], ins["w_nat"]).then_inc(w_in, 16)
                sp.dma_start(a_blk[:], ins["a_blk"]).then_inc(w_in, 16)
                for b in range(NX):
                    sp.dma_start(keep["x_all"][:, b * XB:(b + 1) * XB, :], ins["x"][:, b * XB:(b + 1) * XB, :]).then_inc(x_in[b], 16)
                sp.dma_start(keep["w_h"][:, :, H:H + C], ins["w_t"]).then_inc(w_in, 16)
                sp.dma_start(keep["w_qkv"][:], ins["w_qkv_t"]).then_inc(w_in, 16)
                sp.dma_start(keep["b_qkv"][:], ins["b_qkv"].partition_broadcast(P)).then_inc(w_in, 16)
                sp.dma_start(keep["w_proj"][:], ins["w_proj_t"]).then_inc(w_in, 16)
                sp.dma_start(keep["b_res"][:, 0, :], ins["b_proj"].partition_broadcast(P)).then_inc(w_in, 16)
                sp.dma_start(keep["b_res"][:, 1, :], ins["gnn_bias"].partition_broadcast(P)).then_inc(w_in, 16)
                sp.dma_start(keep["c_out"][:, 0:H], ins["temp"].partition_broadcast(P)).then_inc(w_in, 16)

            @block.gpsimd
            def _(pool):
                nc.gpsimd.memset(keep["ident"][:], 0.0).then_inc(ones_set, 1)
                pool.wait_ge(ones_set, 1)
                nc.gpsimd.affine_select(out=keep["ident"][:], in_=keep["ident"][:], compare_op=ALU.not_equal,
                                        fill=1.0, base=0, pattern=[[-1, P]], channel_multiplier=1).then_inc(consts_made, 1)
                nc.gpsimd.iota(iota_i[:], pattern=[[1, P]], base=0, channel_multiplier=0).then_inc(consts_made, 1)
                nc.gpsimd.iota(iota_pi[:], pattern=[[1, 1]], base=0, channel_multiplier=1).then_inc(consts_made, 1)

            @block.tensor
            def _(pe):
                pe.wait_ge(w_in, 16 * 9)
                for half in range(2):
                    for q in range(2):
                        last = nc.tensor.matmul(ps_fold[:, half, :], w_nat[:, q, half * P:(half + 1) * P],
                                                a_blk[:, q, :], start=(q == 0), stop=(q == 1))
                last.then_inc(folded, 1)

            @block.scalar
            def _(act):
                act.wait_ge(var_made, 1)
                nc.scalar.activation(t1[:], var[:], ACT.Sqrt).then_inc(std_made, 1)

            @block.vector
            def _(dve):
                n = [0]

                def link(ins_):
                    n[0] += 1
                    ins_.then_inc(step, 1)
                    dve.wait_ge(step, n[0])

                nc.vector.memset(keep["c_in"][:, 0:H], QK_SCALE ** 2)
                nc.vector.memset(keep["c_in"][:, H:2 * H], 1.0)
                link(nc.vector.memset(keep["c_out"][:, H:2 * H], QK_SCALE))
                dve.wait_ge(consts_made, 3)
                link(nc.vector.tensor_copy(keep["iota_row"][:], iota_i[:]))
                link(nc.vector.tensor_copy(keep["iota_p"][:], iota_pi[:]))
                link(nc.vector.tensor_scalar(keep["in_range"][:], keep["iota_p"][:], float(N - (NT - 1) * P), None, ALU.is_lt))
                link(nc.vector.tensor_scalar(keep["c_pair"][:], keep["iota_p"][:], float(HD), -0.5 / N, ALU.is_lt, ALU.mult))
                link(nc.vector.tensor_scalar(keep["c_pair"][:], keep["c_pair"][:], 1.0 / N, None, ALU.add))
                for b in range(NX):
                    dve.wait_ge(x_in[b], 16)
                    for i in range(b * XB, (b + 1) * XB):
                        nc.vector.bn_stats(stats[:, i, :], keep["x_all"][:, i, :]).then_inc(stats_made, 1)
                dve.wait_ge(stats_made, NT)
                link(nc.vector.tensor_tensor(t0[:], stats[:, :, 1], stats[:, :, 4], ALU.add))
                link(nc.vector.tensor_scalar(mean[:], t0[:], 0.5, None, ALU.mult))
                link(nc.vector.tensor_tensor(t0[:], stats[:, :, 1], stats[:, :, 4], ALU.subtract))
                link(nc.vector.tensor_tensor(t0[:], t0[:], t0[:], ALU.mult))
                link(nc.vector.tensor_scalar(t0[:], t0[:], 0.25, LN_EPS, ALU.mult, ALU.add))
                link(nc.vector.tensor_tensor(var[:], stats[:, :, 2], stats[:, :, 5], ALU.add))
                nc.vector.scalar_tensor_tensor(out=var[:], in0=var[:], scalar=1.0 / C, in1=t0[:], op0=ALU.mult,
                                               op1=ALU.add).then_inc(var_made, 1)
                dve.wait_ge(w_in, 16 * 9)
                link(nc.vector.tensor_scalar(keep["c_out"][:, 0:H], keep["c_out"][:, 0:H], QK_SCALE ** 2, None, ALU.mult))
                link(nc.vector.tensor_tensor(keep["b_res"][:, 0, :], keep["b_res"][:, 0, :], keep["b_res"][:, 1, :], ALU.add))
                dve.wait_ge(folded, 1)
                nc.vector.tensor_copy(keep["w_h"][:, :, 0:H], ps_fold[:, :, 0:H])
                link(nc.vector.tensor_copy(keep["w_h"][:, :, H + C:ALL_W], ps_fold[:, :, H:2 * H]))
                dve.wait_ge(std_made, 1)
                link(nc.vector.reciprocal(keep["rstd"][:], t1[:]))
                link(nc.vector.scalar_tensor_tensor(out=keep["nmr"][:], in0=mean[:], scalar=-1.0, in1=keep["rstd"][:],
                                                    op0=ALU.mult, op1=ALU.mult))
        s.free()


def turned(t, u, heads, repeat):
    h0, h1 = heads
    a = t[:, u, h0:h1, :]
    return bass.AP(a.tensor, a.offset, [a.ap[0], [EXT, h1 - h0], [0 if repeat else 1, TURNS], [1, AUG]])


def stage_nodes(nc, g, dims, ins, keep, scr):
    NT, N = dims["NT"], dims["N"]
    with ExitStack() as st:
        s = Kit(nc, st, "n_")
        xn = s.sb("xn", [P, 2, C])
        xnT = s.sb("xnT", [P, 2, 2, P])
        hs = s.sb("hs", [P, 2, ALL_W])
        parts = s.sb("parts", [P, 2, 3, DST_W], BF16)
        rest = s.sb("rest", [P, 2, DST_W])
        qk = s.sb("qk", [P, 2, 2 * C])
        sq = s.sb("sq", [P, 2, 2 * C])
        ssq = s.sb("ssq", [P, 2, 2 * H])
        nrm = s.sb("nrm", [P, 2, 2 * H])
        fac = s.sb("fac", [P, 2, 2 * H])
        vv = s.sb("vv", [P, 2, H, VE])
        q2 = s.sb("q2", [P, 2, H, EXT])
        k2 = s.sb("k2", [P, 2, H, EXT])
        prod = s.sb("prod", [P, 2, H, PAIRS])
        zeros = s.sb("zeros", [P, 512])
        gt = s.sb("gt", [P, H // 2, PB * P])
        ps_tv = s.ps("ps_tv", [P, 512])
        ps_t, ps_v = ps_tv[:, 0:C].rearrange("p (c n) -> p c n", c=2), ps_tv[:, C:2 * C]
        ps_h = s.ps("ps_h", [P, 512])
        ps_qk = s.ps("ps_qk", [P, 512])
        REST = PAIRS - 512
        ps_g = [s.ps(f"ps_g{b}", [P, 512]) for b in range(H // 2)]
        ps_r = s.ps("ps_r", [P, 512])

        set_up = s.sem("set_up")
        pool_up = s.sem("pool_up")
        xn_made = s.sem2("xn_made")
        xt_done = s.sem2("xt_done")
        xnT_made = s.sem2("xnT_made")
        proj_done = s.sem2("proj_done")
        hs_made = s.sem2("hs_made")
        part0 = s.sem2("part0")
        rest1 = s.sem2("rest1")
        part1 = s.sem2("part1")
        part2 = s.sem2("part2")
        qk_made = s.sem2("qk_made")
        vv_made = s.sem2("vv_made")
        sq_made = s.sem2("sq_made")
        ssq_raw = s.sem2("ssq_raw")
        ssq_made = s.sem2("ssq_made")
        nrm_made = s.sem2("nrm_made")
        nrm_held = s.sem2("nrm_held")
        fac_raw = s.sem2("fac_raw")
        fac_made = s.sem2("fac_made")
        q_scaled = s.sem2("q_scaled")
        q_made = s.sem2("q_made")
        k_scaled = s.sem2("k_scaled")
        k_made = s.sem2("k_made")
        prod_dve = s.sem2("prod_dve")
        prod_pool = s.sem2("prod_pool")
        summed = s.sem2("summed")
        h_stored = s.sem2("h_stored")
        d_stored = s.sem2("d_stored")
        q_stored = s.sem2("q_stored")
        masked = s.sem("masked")
        g_put = s.sem("g_put")
        g_turned = s.sem("g_turned")
        g_scaled = s.sem("g_scaled")

        with nc.Block() as block:
            @block.scalar
            def _(act):
                def normalise(i, k, u):
                    freed(act, xt_done, k, u)
                    nc.scalar.activation(xn[:, u, :], keep["x_all"][:, bass.ds(i, 1), :], ACT.Identity,
                                         scale=keep["rstd"][:, bass.ds(i, 1)], bias=keep["nmr"][:, bass.ds(i, 1)]).then_inc(xn_made[u], 1)

                def put(i, k, u):
                    ready(act, xt_done, k, u)
                    freed(act, proj_done, k, u)
                    nc.scalar.copy(xnT[:, u], ps_t).then_inc(xnT_made[u], 1)

                def rest_of(i, k, u):
                    ready(act, proj_done, k, u)
                    freed(act, h_stored, k, u, 16)
                    freed(act, rest1, k, u)
                    nc.scalar.copy(hs[:, u, :], ps_h[:, 0:ALL_W]).then_inc(hs_made[u], 1)
                    ready(act, hs_made, k, u)
                    freed(act, d_stored, k, u, 16)
                    nc.scalar.copy(parts[:, u, 0, :], hs[:, u, H:ALL_W]).then_inc(part0[u], 1)
                    ready(act, qk_made, k, u)
                    freed(act, ssq_raw, k, u)
                    nc.scalar.activation(sq[:, u, :], qk[:, u, :], ACT.Square).then_inc(sq_made[u], 1)
                    ready(act, ssq_made, k, u)
                    freed(act, nrm_held, k, u)
                    nc.scalar.activation(nrm[:, u, :], ssq[:, u, :], ACT.Sqrt).then_inc(nrm_made[u], 1)

                def step(a, b):
                    if a:
                        normalise(*a)
                    if b:
                        rest_of(*b)
                    if a:
                        put(*a)

                woven(act, NT, step)

            @block.tensor
            def _(pe):
                pe.wait_ge(set_up, 1)
                for bank in ps_g + [ps_r]:
                    nc.tensor.matmul(bank[:], zeros[:, 0:P], zeros[:], start=True, stop=True, skip_group_check=True)

                def project(i, k, u):
                    ready(pe, xn_made, k, u)
                    before(pe, xnT_made, k, u)
                    before(pe, vv_made, k, u)
                    for c in range(2):
                        last = nc.tensor.transpose(ps_t[:, c, :], xn[:, u, c * P:(c + 1) * P], keep["ident"][:])
                    last.then_inc(xt_done[u], 1)
                    ready(pe, xnT_made, k, u)
                    before(pe, hs_made, k, u)
                    before(pe, qk_made, k, u)
                    for out, w in ((ps_h[:, 0:ALL_W], keep["w_h"][:, :, :]), (ps_qk[:], keep["w_qkv"][:, :, 0:2 * C]),
                                   (ps_v, keep["w_qkv"][:, :, 2 * C:3 * C])):
                        for c in range(2):
                            last = nc.tensor.matmul(out, xnT[:, u, c, :], w[:, c, :], start=(c == 0), stop=(c == 1))
                    last.then_inc(proj_done[u], 1)

                def sum_products(i, k, u):
                    ready(pe, vv_made, k, u)
                    if isinstance(i, int) and i == NT - 1:
                        pe.wait_ge(masked, 1)
                    for h in range(H):
                        if h == 0:
                            ready(pe, prod_dve, k, u)
                        if h == H - POOL_HEADS:
                            ready(pe, prod_pool, k, u)
                        b, lo = h % (H // 2), h // (H // 2) * 64
                        for out, x in ((ps_g[b][lo:lo + VE, :], prod[:, u, h, 0:512]),
                                       (ps_r[lo:lo + VE, b * REST:(b + 1) * REST], prod[:, u, h, 512:PAIRS])):
                            last = nc.tensor.matmul(out, vv[:, u, h, :], x, start=False, stop=True, skip_group_check=True)
                    last.then_inc(summed[u], 1)

                skewed(pe, NT, project, sum_products)
                pe.wait_ge(g_put, H // 2 + 1)
                for b in range(PB):
                    wait(pe, g_scaled, 2 * b)
                    for m in range(H // 2):
                        last = nc.tensor.transpose(ps_qk[:, m * P:(m + 1) * P], gt[:, m, b * P:(b + 1) * P], keep["ident"][:])
                    last.then_inc(g_turned, 1)

            @block.vector
            def _(dve):
                nc.vector.memset(vv[:, :, :, 0:1], 1.0)
                nc.vector.memset(q2[:, :, :, HD:AUG], QK_SCALE)
                nc.vector.memset(k2[:, :, :, HD:AUG], QK_SCALE)
                nc.vector.memset(gt[:, :, PAIRS:PB * P], 0.0)
                nc.vector.memset(zeros[:], 0.0).then_inc(set_up, 1)
                dve.wait_ge(set_up, 1)

                def body(i, k, u):
                    ready(dve, proj_done, k, u)
                    freed(dve, q_scaled, k, u)
                    freed(dve, k_scaled, k, u)
                    freed(dve, sq_made, k, u)
                    nc.vector.tensor_tensor(qk[:, u, :], ps_qk[:], keep["b_qkv"][:, 0:2 * C], ALU.add).then_inc(qk_made[u], 1)
                    freed(dve, summed, k, u)
                    nc.vector.tensor_tensor(vv[:, u, :, 1:VE], ps_v.rearrange("p (h d) -> p h d", h=H),
                                            keep["b_qkv"][:, 2 * C:3 * C].rearrange("p (h d) -> p h d", h=H),
                                            ALU.add).then_inc(vv_made[u], 1)
                    if isinstance(i, int) and i == NT - 1:
                        ready(dve, vv_made, k, u)
                        nc.vector.tensor_scalar(vv[:, u], vv[:, u], keep["in_range"][:, 0:1], None, ALU.mult).then_inc(masked, 1)
                    ready(dve, part0, k, u)
                    freed(dve, part2, k, u)
                    nc.vector.tensor_tensor(rest[:, u, :], hs[:, u, H:ALL_W], parts[:, u, 0, :], ALU.subtract).then_inc(rest1[u], 1)
                    ready(dve, sq_made, k, u)
                    freed(dve, nrm_made, k, u)
                    nc.vector.reduce_sum(ssq[:, u, :], sq[:, u, :].rearrange("p (h d) -> p h d", d=HD), AX).then_inc(ssq_raw[u], 1)
                    ready(dve, rest1, k, u)
                    nc.vector.tensor_copy(parts[:, u, 1, :], rest[:, u, :]).then_inc(part1[u], 1)
                    ready(dve, ssq_raw, k, u)
                    nc.vector.tensor_tensor(ssq[:, u, :], ssq[:, u, :], keep["c_in"][:], ALU.mult).then_inc(ssq_made[u], 1)
                    ready(dve, part1, k, u)
                    nc.vector.tensor_tensor(parts[:, u, 2, :], rest[:, u, :], parts[:, u, 1, :], ALU.subtract).then_inc(part2[u], 1)
                    ready(dve, nrm_made, k, u)
                    nc.vector.tensor_scalar(fac[:, u, :], nrm[:, u, :], NORM_EPS, None, ALU.max).then_inc(nrm_held[u], 1)
                    ready(dve, nrm_held, k, u)
                    nc.vector.reciprocal(fac[:, u, :], fac[:, u, :]).then_inc(fac_raw[u], 1)
                    ready(dve, fac_raw, k, u)
                    nc.vector.tensor_tensor(fac[:, u, :], fac[:, u, :], keep["c_out"][:], ALU.mult).then_inc(fac_made[u], 1)
                    ready(dve, fac_made, k, u)
                    freed(dve, prod_pool, k, u)
                    for which, dst, scaled in ((1, k2, k_scaled), (0, q2, q_scaled)):
                        if which == 0:
                            freed(dve, q_stored, k, u, 16)
                        nc.vector.tensor_tensor(dst[:, u, :, 0:HD],
                                                qk[:, u, which * C:(which + 1) * C].rearrange("p (h d) -> p h d", h=H),
                                                fac[:, u, which * H:(which + 1) * H].unsqueeze(2).to_broadcast([P, H, HD]),
                                                ALU.mult).then_inc(scaled[u], 1)
                    ready(dve, k_scaled, k, u)
                    nc.vector.tensor_copy(k2[:, u, :, AUG:EXT], k2[:, u, :, 0:TURNS - 1]).then_inc(k_made[u], 1)
                    ready(dve, q_scaled, k, u)
                    nc.vector.tensor_copy(q2[:, u, :, AUG:EXT], q2[:, u, :, 0:TURNS - 1]).then_inc(q_made[u], 1)
                    ready(dve, k_made, k, u)
                    hv = (0, H - POOL_HEADS)
                    nc.vector.tensor_tensor(prod[:, u, hv[0]:hv[1], 0:PAIRS].rearrange("p h (r i) -> p h r i", i=AUG),
                                            turned(k2, u, hv, True), turned(k2, u, hv, False), ALU.mult).then_inc(prod_dve[u], 1)

                pairs(dve, NT, body)
                ready(dve, summed, NT // 2, 0)
                for m in range(H // 2):
                    nc.vector.tensor_copy(gt[:, m, 0:512], ps_g[m][:]).then_inc(g_put, 1)
                nc.vector.tensor_copy(gt[:, :, 512:PAIRS], ps_r[:, 0:H // 2 * REST].rearrange("p (m r) -> p m r", r=REST)).then_inc(g_put, 1)
                g_sum = keep["g_sum"][:].rearrange("p (f m b) e -> p f m b e", f=2, b=PB)
                for b in range(PB):
                    dve.wait_ge(g_turned, b + 1)
                    w = keep["c_pair"][:, 0:1] if b == 0 else 1.0 / N
                    for f in range(2):
                        src = ps_qk[:].rearrange("p (m c) -> p m c", c=P)[:, :, f * 64:f * 64 + VE]
                        nc.vector.tensor_scalar(g_sum[:, f, :, b, :], src, w, None, ALU.mult).then_inc(g_scaled, 1)

            @block.gpsimd
            def _(pool):
                pool.wait_ge(set_up, 1)

                def body(i, k, u):
                    ready(pool, hs_made, k, u)
                    pool.dma_start(row(scr["src_rows"], i).rearrange("o p w -> p (o w)"), hs[:, u, 0:SRC_W]).then_inc(h_stored[u], 16)
                    ready(pool, part2, k, u)
                    pool.dma_start(row(scr["dst_parts"], i).rearrange("o p w -> p (o w)"),
                                   parts[:, u].rearrange("p a w -> p (a w)")).then_inc(d_stored[u], 16)
                    ready(pool, k_made, k, u)
                    freed(pool, summed, k, u)
                    hv = (H - POOL_HEADS, H)
                    nc.gpsimd.tensor_tensor(prod[:, u, hv[0]:hv[1], 0:PAIRS].rearrange("p h (r i) -> p h r i", i=AUG),
                                            turned(k2, u, hv, True), turned(k2, u, hv, False), ALU.mult).then_inc(prod_pool[u], 1)
                    ready(pool, q_made, k, u)
                    pool.dma_start(row(scr["q_rows"], i).rearrange("o p w -> p (o w)"),
                                   q2[:, u].rearrange("p h e -> p (h e)")).then_inc(q_stored[u], 16)

                pairs(pool, NT, body)
                for sem in (h_stored, d_stored, q_stored):
                    pool.wait_ge(sem[0], 16 * (NT // 2 + 1))
                    pool.wait_ge(sem[1], 16 * (NT // 2))
        s.free()


def stage_mix(nc, g, dims, ins, keep, scr):
    NT = dims["NT"]
    with ExitStack() as st:
        s = Kit(nc, st, "m_")
        q2 = s.sb("q2", [P, 2, H, EXT])
        prod = s.sb("prod", [P, 2, H, PB * P])
        prodT = s.sb("prodT", [P, 2, PB, P])
        ry = s.sb("ry", [P, 2, H])
        yn = s.sb("yn", [P, 2, C])
        ynT = s.sb("ynT", [P, 2, 2, P])
        xb = s.sb("xb", [P, 2, C])
        res = s.sb("res", [P, 2, C])
        ps_p = [s.ps(f"ps_p{b}", [P, 8, P]) for b in range(2)]
        ps_w = s.ps("ps_w", [P, H // 2, P])
        ps_y = s.ps("ps_y", [P, H // 2, P])
        yw = s.sb("yw", [P, 2, H // 2, P])
        zeros = s.sb("zeros", [P, 512])
        ps_yt = s.ps("ps_yt", [P, 2, P])
        ps_o = s.ps("ps_o", [P, C])
        set_up = s.sem("set_up")
        q_in = s.sem2("q_in")
        prod_dve = s.sem2("prod_dve")
        prod_pool = s.sem2("prod_pool")
        turned_t = s.sem2("turned_t")
        prodT_made = s.sem2("prodT_made")
        head_done = s.sem2("head_done")
        yw_made = s.sem2("yw_made")
        y_done = s.sem2("y_done")
        zeros_set = s.sem("zeros_set")
        ry_made = s.sem2("ry_made")
        yn_made = s.sem2("yn_made")
        yt_done = s.sem2("yt_done")
        ynT_made = s.sem2("ynT_made")
        o_done = s.sem2("o_done")
        xb_made = s.sem2("xb_made")
        res_made = s.sem2("res_made")
        res_stored = s.sem2("res_stored")
        HH = H // 2

        with nc.Block() as block:
            @block.sync
            def _(sp):
                def load(i, k, u):
                    freed(sp, prod_dve, k, u)
                    freed(sp, prod_pool, k, u)
                    sp.dma_start(q2[:, u].rearrange("p h e -> p (h e)"), row(scr["q_rows"], i).rearrange("o p w -> p (o w)")).then_inc(q_in[u], 16)

                pairs(sp, NT, load)

            @block.gpsimd
            def _(pool):
                nc.gpsimd.memset(prod[:, :, :, PAIRS:PB * P], 0.0).then_inc(set_up, 1)

                def products(i, k, u):
                    ready(pool, q_in, k, u, 16)
                    freed(pool, yn_made, k, u)
                    hv = (H - POOL_HEADS, H)
                    nc.gpsimd.tensor_tensor(prod[:, u, hv[0]:hv[1], 0:PAIRS].rearrange("p h (r i) -> p h r i", i=AUG),
                                            turned(q2, u, hv, True), turned(q2, u, hv, False), ALU.mult).then_inc(prod_pool[u], 1)
                    freed(pool, res_made, k, u)
                    nc.gpsimd.tensor_tensor(xb[:, u, :], keep["x_all"][:, bass.ds(i, 1), :].rearrange("p o c -> p (o c)"),
                                            keep["b_res"][:, 0, :], ALU.add).then_inc(xb_made[u], 1)

                def store(i, k, u):
                    ready(pool, res_made, k, u)
                    pool.dma_start(row(scr["x_mix"], i).rearrange("o p w -> p (o w)"), res[:, u, :]).then_inc(res_stored[u], 16)

                led(pool, NT, none, products, store)
                pool.wait_ge(res_stored[0], 16 * (NT // 2 + 1))
                pool.wait_ge(res_stored[1], 16 * (NT // 2))

            @block.vector
            def _(dve):
                def products(i, k, u):
                    ready(dve, q_in, k, u, 16)
                    freed(dve, yn_made, k, u)
                    hv = (0, H - POOL_HEADS)
                    nc.vector.tensor_tensor(prod[:, u, hv[0]:hv[1], 0:PAIRS].rearrange("p h (r i) -> p h r i", i=AUG),
                                            turned(q2, u, hv, True), turned(q2, u, hv, False), ALU.mult).then_inc(prod_dve[u], 1)

                def divide(i, k, u):
                    ready(dve, y_done, k, u)
                    freed(dve, yn_made, k, u)
                    nc.vector.reciprocal(ry[:, u, :].rearrange("p (f m) -> p m f", f=2), halves[:, :, :, 0]).then_inc(ry_made[u], 1)
                    ready(dve, ry_made, k, u)
                    freed(dve, yt_done, k, u)
                    for f in range(2):
                        last = nc.vector.tensor_tensor(yn[:, u, f * C // 2:(f + 1) * C // 2].rearrange("p (m d) -> p m d", d=HD), halves[:, :, f, 1:VE],
                                                       ry[:, u, f * HH:(f + 1) * HH].unsqueeze(2).to_broadcast([P, HH, HD]), ALU.mult)
                    last.then_inc(yn_made[u], 1)

                def finish(i, k, u):
                    ready(dve, o_done, k, u)
                    ready(dve, xb_made, k, u)
                    freed(dve, res_stored, k, u, 16)
                    nc.vector.tensor_tensor(res[:, u, :], ps_o[:], xb[:, u, :], ALU.add).then_inc(res_made[u], 1)

                halves = ps_y[:].rearrange("p m (f c) -> p m f c", f=2)
                nc.vector.memset(zeros[:], 0.0).then_inc(zeros_set, 1)
                led(dve, NT, divide, products, finish)

            @block.scalar
            def _(act):
                def put(h, i, k, u):
                    n = HH * i + h // 2
                    act.wait_ge(turned_t[h % 2], n + 1)
                    wait(act, head_done[h % 2], n)
                    nc.scalar.copy(prodT[:, h % 2], ps_p[h % 2][:, 0:PB, :]).then_inc(prodT_made[h % 2], 1)

                def put_y(i, k, u):
                    act.wait_ge(head_done[1], HH * (i + 1))
                    freed(act, y_done, k, u)
                    nc.scalar.copy(yw[:, u], ps_w[:]).then_inc(yw_made[u], 1)

                def put_yn(i, k, u):
                    ready(act, yt_done, k, u)
                    freed(act, o_done, k, u)
                    nc.scalar.copy(ynT[:, u], ps_yt[:]).then_inc(ynT_made[u], 1)

                def step(a, b):
                    if b:
                        put_y(*b)
                    for h in range(H):
                        if a:
                            put(h, *a)
                        if b and h == 4:
                            put_yn(*b)

                woven(act, NT, step)

            @block.tensor
            def _(pe):
                pe.wait_ge(set_up, 1)
                pe.wait_ge(zeros_set, 1)
                nc.tensor.matmul(ps_w[:].rearrange("p m n -> p (m n)"), zeros[:, 0:P], zeros[:], start=True, stop=True, skip_group_check=True)

                def turn(h, i, k, u):
                    n = HH * i + h // 2
                    if h == 0:
                        ready(pe, prod_dve, k, u)
                    if h == H - POOL_HEADS:
                        ready(pe, prod_pool, k, u)
                    wait(pe, prodT_made[h % 2], n)
                    for b in range(PB):
                        last = nc.tensor.transpose(ps_p[h % 2][:, b, :], prod[:, u, h, b * P:(b + 1) * P], keep["ident"][:])
                    last.then_inc(turned_t[h % 2], 1)

                def weigh(h, i, k, u):
                    n = HH * i + h // 2
                    pe.wait_ge(prodT_made[h % 2], n + 1)
                    if h == 0:
                        before(pe, yw_made, k, u)
                    lo = h // HH * 64
                    for b in range(PB):
                        last = nc.tensor.matmul(ps_w[lo:lo + VE, h % HH, :], keep["g_sum"][:, h * PB + b, :], prodT[:, h % 2, b, :],
                                                start=(b == 0), stop=(b == PB - 1), skip_group_check=True)
                    last.then_inc(head_done[h % 2], 1)

                def turn_back(i, k, u):
                    ready(pe, yw_made, k, u)
                    before(pe, yn_made, k, u)
                    for m in range(HH):
                        last = nc.tensor.transpose(ps_y[:, m, :], yw[:, u, m, :], keep["ident"][:])
                    last.then_inc(y_done[u], 1)

                def turn_yn(i, k, u):
                    ready(pe, yn_made, k, u)
                    for c in range(2):
                        last = nc.tensor.transpose(ps_yt[:, c, :], yn[:, u, c * P:(c + 1) * P], keep["ident"][:])
                    last.then_inc(yt_done[u], 1)

                def project(i, k, u):
                    ready(pe, ynT_made, k, u)
                    before(pe, res_made, k, u)
                    for c in range(2):
                        last = nc.tensor.matmul(ps_o[:], ynT[:, u, c, :], keep["w_proj"][:, c, :], start=(c == 0), stop=(c == 1))
                    last.then_inc(o_done[u], 1)

                def step(a, b):
                    for h in range(H):
                        if a:
                            turn(h, *a)
                        if b and h == 1:
                            turn_back(*b)
                        if a and h > 0:
                            weigh(h - 1, *a)
                        if b and h == 4:
                            turn_yn(*b)
                        if b and h == 6:
                            project(*b)
                    if a:
                        weigh(H - 1, *a)

                woven(pe, NT, step)
        s.free()



def plan_dims(N, E):
    NT = -(-N // P)
    T = -(-E // GE)
    S = T + NT - 1
    S += (-S) % 4
    assert NT % 2 == 1 and NT % 7 == 0 and E < T * GE and S <= 512 and T <= 512
    return dict(N=N, E=E, NT=NT, T=T, S=S)


def lay_out(a):
    a = {n: np.asarray(v) for n, v in a.items()}
    N, E = a["x"].shape[0], a["src"].shape[0]
    d = plan_dims(N, E)
    NT, T = d["NT"], d["T"]

    def halves(w):
        return np.ascontiguousarray(w.reshape(2, P, -1).transpose(1, 0, 2))

    def cols(v):
        return np.ascontiguousarray(v.reshape(EXPERTS, 2, P).transpose(2, 0, 1))

    o = {}
    x = np.zeros((NT * P, C), np.float32)
    x[:N] = a["x"]
    o["x"] = np.ascontiguousarray(x.reshape(NT, P, C).transpose(1, 0, 2))
    blk = np.zeros((C, 2 * H), np.float32)
    for h in range(H):
        blk[h * HD:(h + 1) * HD, h] = a["L0_gnn_a_src"][h]
        blk[h * HD:(h + 1) * HD, H + h] = a["L0_gnn_a_dst"][h]
    o["a_blk"] = halves(blk)
    o["w_nat"] = halves(a["L0_gnn_W"])
    o["w_t"] = halves(a["L0_gnn_W"].T)
    o["w_qkv_t"] = halves(a["L0_mix_Wqkv"].T)
    o["b_qkv"] = a["L0_mix_bqkv"]
    o["w_proj_t"] = halves(a["L0_mix_Wproj"].T)
    o["b_proj"] = a["L0_mix_bproj"]
    o["gnn_bias"] = a["L0_gnn_bias"]
    o["temp"] = a["L0_mix_temperature"].reshape(H)
    dst = np.full(T * GE, 1 << 20, np.int32)
    dst[:E] = a["dst"]
    src = np.zeros(T * GE, np.int32)
    src[:E] = a["src"]
    prev = np.full(T * GE, -1, np.int32)
    prev[1:] = dst[:-1]
    o["dst_rows"] = np.concatenate([prev.reshape(T, GE)[:, :1], dst.reshape(T, GE)], axis=1)
    o["group_last"] = np.ascontiguousarray(dst.reshape(T, GE)[:, GE - 1:])
    o["src_in"] = src.reshape(T, GE)
    ea = np.zeros((T * GE, EF), np.float32)
    ea[:E] = a["edge_attr_3"]
    o["edge_f"] = np.ascontiguousarray(ea.T).reshape(P, -1)
    o["w_edge"] = np.concatenate([a["L0_gnn_edge_W"].T, a["L0_gnn_edge_b"][None]], axis=0)
    for n in ("W1", "W2", "Wo"):
        o[n] = np.ascontiguousarray(a["L0_ffn_" + n].reshape(EXPERTS, 2, P, C).transpose(2, 0, 1, 3))
    for n in ("b1", "g1", "be1", "m1", "v1", "b2", "g2", "be2", "m2", "v2"):
        o[n] = cols(a["L0_ffn_" + n])
    o["Wr"] = halves(a["L0_ffn_Wr"])
    o["br"] = a["L0_ffn_br"]
    bo = np.zeros((P // EXPERTS, EXPERTS, P // EXPERTS, C), np.float32)
    for b in range(P // EXPERTS):
        bo[b, :, b, :] = a["L0_ffn_bo"]
    o["bo_blocks"] = bo.reshape(P, P // EXPERTS, C)
    return o, d


def stage_plan(nc, dims, ins, keep, scr):
    NT, T, S = dims["NT"], dims["T"], dims["S"]
    TB = -(-T // P)
    SB = 4
    with ExitStack() as st:
        s = Kit(nc, st, "p_")
        steps_i = s.sb("steps_i", [P, GE], I32)
        steps = s.sb("steps", [P, GE])
        scol_i = s.sb("scol_i", [P, SB], I32)
        scol = s.sb("scol", [P, SB])
        ones = s.sb("ones", [P, P])
        last_i = s.sb("last_i", [P, TB], I32)
        last_f = s.sb("last_f", [P, TB])
        thr = s.sb("thr", [P, NT])
        less = s.sb("less", [P, TB, NT])
        f = s.sb("f", [NT, 1])
        f1 = s.sb("f1", [NT, 1])
        past = s.sb("past", [NT, GE])
        jrow = s.sb("jrow", [P, GE])
        trow = s.sb("trow", [1, GE])
        jcol = s.sb("jcol", [P, SB])
        j128 = s.sb("j128", [P, SB])
        tcol = s.sb("tcol", [P, SB])
        tcol_i = s.sb("tcol_i", [P, SB], I32)
        dst_g = s.sb("dst_g", [P, SB, GE + 1], I32)
        src_g = s.sb("src_g", [P, SB, GE], I32)
        rel = s.sb("rel", [P, SB, GE + 1])
        srcf = s.sb("srcf", [P, SB, GE])
        begin = s.sb("begin", [P, SB, GE])
        pen_b = s.sb("pen_b", [P, SB, GE], BF16)
        rel_b = s.sb("rel_b", [P, SB, GE], BF16)
        FW = EF * T * GE // P
        feats = s.sb("feats", [P, FW])
        f_parts = s.sb("f_parts", [P, 3, FW], BF16)
        f_in = s.sem("f_in")
        f_split = s.sem("f_split")
        f_stored = s.sem("f_stored")
        ps_e = s.ps("ps_e", [NT, 1])
        ps_j = s.ps("ps_j", [P, GE])
        ps_jc = s.ps("ps_jc", [P, SB])
        ps_t = [s.ps(f"ps_t{u}", [P, TG, P]) for u in range(2)]
        l_in = s.sem("l_in")
        iotas = s.sem("iotas")
        step = s.sem("step")
        less_made = s.sem("less_made")
        e_done = s.sem("e_done")
        f_made = s.sem("f_made")
        past_made = s.sem("past_made")
        j_done = s.sem("j_done")
        tcol_made = s.sem("tcol_made")
        dst_in = s.sem("dst_in")
        src_in = s.sem("src_in")
        rel_made = s.sem("rel_made")
        srcf_made = s.sem("srcf_made")
        bf_made = s.sem("bf_made")
        turned_ = s.sem("turned")
        put = s.sem("put")
        stored = s.sem("stored")
        with nc.Block() as block:
            @block.sync
            def _(sp):
                for b in range(TB):
                    n = min(P, T - b * P)
                    sp.dma_start(last_i[0:n, b:b + 1], ins["group_last"][b * P:b * P + n, :]).then_inc(l_in, 16)
                sp.dma_start(feats[:], ins["edge_f"]).then_inc(f_in, 16)
                for n, (part, _) in enumerate(PRODUCTS):
                    sp.wait_ge(f_split, part + 1)
                    sp.dma_start(scr["edge_parts"][n * EF:(n + 1) * EF].rearrange("f t e -> (f t e)").rearrange("(p w) -> p w", p=P),
                                 f_parts[:, part, :]).then_inc(f_stored, 16)
                sp.wait_ge(f_stored, 16 * len(PRODUCTS))
                sp.wait_ge(bf_made, 2)
                sp.dma_start(scr["rel_rows"].rearrange("(b p) e -> p b e", p=P), rel_b[:]).then_inc(stored, 16)
                sp.dma_start(scr["pen_rows"].rearrange("(b p) e -> p b e", p=P), pen_b[:]).then_inc(stored, 16)
                sp.wait_ge(stored, 32)

            @block.gpsimd
            def _(pool):
                nc.gpsimd.iota(steps_i[:], pattern=[[1, GE]], base=0, channel_multiplier=0).then_inc(iotas, 1)
                nc.gpsimd.iota(scol_i[:], pattern=[[P, SB]], base=0, channel_multiplier=1).then_inc(iotas, 1)
                pool.wait_ge(tcol_made, 1)
                for b in range(SB):
                    idx = bass.IndirectOffsetOnAxis(ap=tcol_i[:, b:b + 1], axis=0)
                    pool.indirect_dma_start(out=dst_g[:, b, :], out_offset=None, in_=ins["dst_rows"], in_offset=idx).then_inc(dst_in, 16)
                    pool.indirect_dma_start(out=src_g[:, b, :], out_offset=None, in_=ins["src_in"], in_offset=idx).then_inc(src_in, 16)

            @block.tensor
            def _(pe):
                pe.wait_ge(less_made, TB)
                for b in range(TB):
                    n = min(P, T - b * P)
                    last = nc.tensor.matmul(ps_e[:], less[0:n, b, :], ones[0:n, 0:1], start=(b == 0), stop=(b == TB - 1))
                last.then_inc(e_done, 1)
                pe.wait_ge(past_made, 1)
                nc.tensor.matmul(ps_j[:], ones[0:NT, :], past[:], start=True, stop=True)
                for b in range(SB):
                    last = nc.tensor.matmul(ps_jc[:, b:b + 1], past[:, b * P:(b + 1) * P], ones[0:NT, 0:1], start=True, stop=True)
                last.then_inc(j_done, 1)
                for n in range(2 * SB):
                    b, src = n // 2, n % 2
                    if src:
                        pe.wait_ge(srcf_made, b + 1)
                    else:
                        pe.wait_ge(rel_made, b + 1)
                    if n >= 2:
                        pe.wait_ge(put, n - 1)
                    for t in range(TG):
                        v = srcf[:, b, t * P:(t + 1) * P] if src else rel[:, b, 1 + t * P:1 + (t + 1) * P]
                        last = nc.tensor.transpose(ps_t[n % 2][:, t, :], v, keep["ident"][:])
                    last.then_inc(turned_, 1)

            @block.vector
            def _(dve):
                n = [0]

                def link(ins_):
                    n[0] += 1
                    ins_.then_inc(step, 1)
                    dve.wait_ge(step, n[0])

                dve.wait_ge(iotas, 2)
                link(nc.vector.memset(ones[:], 1.0))
                link(nc.vector.tensor_copy(steps[:], steps_i[:]))
                link(nc.vector.tensor_copy(scol[:], scol_i[:]))
                link(nc.vector.tensor_scalar(thr[:], steps[:, 0:NT], float(P), float(P), ALU.mult, ALU.add))
                dve.wait_ge(l_in, 16 * TB)
                for b in range(TB):
                    m = min(P, T - b * P)
                    link(nc.vector.tensor_copy(last_f[0:m, b:b + 1], last_i[0:m, b:b + 1]))
                    nc.vector.tensor_scalar(less[0:m, b, :], thr[0:m, :], last_f[0:m, b:b + 1], None, ALU.is_gt).then_inc(less_made, 1)
                dve.wait_ge(e_done, 1)
                link(nc.vector.tensor_scalar(f1[:], ps_e[:], float(T - 1), 1.0, ALU.min, ALU.add))
                nc.vector.tensor_tensor(f[:], f1[:], keep["iota_p"][0:NT, :], ALU.add).then_inc(f_made, 1)
                dve.wait_ge(f_made, 1)
                nc.vector.tensor_scalar(past[:], steps[0:NT, :], f[:, 0:1], None, ALU.is_ge).then_inc(past_made, 1)
                dve.wait_ge(j_done, 1)
                link(nc.vector.tensor_copy(jrow[:], ps_j[:]))
                link(nc.vector.tensor_copy(jcol[:], ps_jc[:]))
                link(nc.vector.tensor_tensor(tcol[:], scol[:], jcol[:], ALU.subtract))
                nc.vector.tensor_scalar(tcol_i[:], tcol[:], float(T - 1), None, ALU.min).then_inc(tcol_made, 1)
                link(nc.vector.tensor_scalar(j128[:], jcol[:], float(P), None, ALU.mult))
                link(nc.vector.tensor_tensor(trow[:], steps[0:1, :], jrow[0:1, :], ALU.subtract))
                nc.vector.tensor_scalar(keep["t_of"][:], trow[:, 0:S], float(T - 1), None, ALU.min)
                nc.vector.tensor_scalar(keep["j_of"][:], jrow[0:1, 0:S], float(NT - 1), None, ALU.min)
                dve.wait_ge(f_in, 16)
                for part in range(3):
                    nc.vector.tensor_copy(f_parts[:, part, :], feats[:]).then_inc(f_split, 1)
                    if part < 2:
                        dve.wait_ge(f_split, part + 1)
                        link(nc.vector.tensor_tensor(feats[:], feats[:], f_parts[:, part, :], ALU.subtract))
                dve.wait_ge(dst_in, 16 * SB)
                dve.wait_ge(src_in, 16 * SB)
                for b in range(SB):
                    link(nc.vector.tensor_scalar(rel[:, b, :], dst_g[:, b, :], j128[:, b:b + 1], None, ALU.subtract))
                    nc.vector.tensor_scalar(rel[:, b, :], rel[:, b, :], -1.0, float(P), ALU.max, ALU.min).then_inc(rel_made, 1)
                    nc.vector.tensor_copy(srcf[:, b, :], src_g[:, b, :]).then_inc(srcf_made, 1)
                dve.wait_ge(rel_made, SB)
                link(nc.vector.tensor_tensor(begin[:], rel[:, :, 1:GE + 1], rel[:, :, 0:GE], ALU.not_equal))
                nc.vector.tensor_scalar(pen_b[:], begin[:], NEG, None, ALU.mult).then_inc(bf_made, 1)
                nc.vector.tensor_copy(rel_b[:], rel[:, :, 1:GE + 1]).then_inc(bf_made, 1)
                for m in range(2 * SB):
                    b, src = m // 2, m % 2
                    dve.wait_ge(turned_, m + 1)
                    out = keep["idx_e"] if src else keep["rel_e"]
                    nc.vector.tensor_copy(out[:, b * P:(b + 1) * P, :].rearrange("p s t -> p t s"), ps_t[m % 2][:]).then_inc(put, 1)
        s.free()


def stage_scores(nc, dims, ins, keep, scr):
    S = dims["S"]
    HT = TG // 2
    R = 4
    with ExitStack() as st:
        s = Kit(nc, st, "s_")
        FR = 3 + EF * len(PRODUCTS)
        w_edge = s.sb("w_edge", [EF + 1, C])
        w_rest = s.sb("w_rest", [EF + 1, C])
        w_parts = s.sb("w_parts", [EF + 1, 3, C], BF16)
        w_rows = s.sb("w_rows", [FR, C], BF16)
        table = s.sb("table", [P, R, 3, DST_W], BF16)
        feat = s.sb("feat", [FR, R, GE], BF16)
        relb = s.sb("relb", [P, R, GE], BF16)
        hot = s.sb("hot", [P, R, GE], BF16)
        idx = s.sb("idx", [P, R, TG], I32)
        rows = s.sb("rows", [P, R, TG, SRC_W])
        enc = s.sb("enc", [P, 2, HT, C])
        prod = s.sb("prod", [P, 2, HT, C])
        tmp = s.sb("tmp", [P, 2, HT, H])
        red = s.sb("red", [P, 2, HT, H])
        ps_f = [s.ps(f"ps_f{h}", [P, HT, C]) for h in range(2)]
        ps_d = [s.ps(f"ps_d{h}", [P, HT, 512]) for h in range(2)]
        w_in = s.sem("w_in")
        w_split = s.sem("w_split")
        w_left = s.sem("w_left")
        w_laid = s.sem("w_laid")
        ones_set = s.sem("ones_set")
        table_in = s.sem2("table_in", R)
        feat_in = s.sem2("feat_in", R)
        rel_in = s.sem2("rel_in", R)
        passed = s.sem("passed")
        rows_in = s.sem2("rows_in", R)
        rows_kept = s.sem2("rows_kept", R)
        idx_made = s.sem2("idx_made", R)
        hot_made = s.sem2("hot_made", R)
        feat_done = [s.sem2("feat_done_a", R), s.sem2("feat_done_b", R)]
        enc_made = [s.sem2("enc_made_a", R), s.sem2("enc_made_b", R)]
        spread = [s.sem2("spread_a", R), s.sem2("spread_b", R)]
        multiplied = [s.sem2("multiplied_a", R), s.sem2("multiplied_b", R)]
        tmp_made = [s.sem2("tmp_made_a", R), s.sem2("tmp_made_b", R)]
        reduced = [s.sem2("reduced_a", R), s.sem2("reduced_b", R)]
        scored = [s.sem2("scored_a", R), s.sem2("scored_b", R)]

        with nc.Block() as block:
            @block.sync
            def _(sp):
                sp.dma_start(w_edge[:], ins["w_edge"]).then_inc(w_in, 16)
                sp.wait_ge(w_split, 3)
                for part in range(3):
                    sp.dma_start(w_rows[part:part + 1, :], w_parts[EF:EF + 1, part, :]).then_inc(w_laid, 16)
                for n, (_, part) in enumerate(PRODUCTS):
                    sp.dma_start(w_rows[3 + n * EF:3 + (n + 1) * EF, :], w_parts[0:EF, part, :]).then_inc(w_laid, 16)

                def load(i, k, u):
                    t = sp.value_load(keep["t_of"][0:1, bass.ds(i, 1)], min_val=0, max_val=dims["T"] - 1)
                    j = sp.value_load(keep["j_of"][0:1, bass.ds(i, 1)], min_val=0, max_val=dims["NT"] - 1)
                    freed(sp, hot_made, k, u)
                    sp.dma_start(relb[:, u, :], row(scr["rel_rows"], i).to_broadcast([P, GE])).then_inc(rel_in[u], 16)
                    freed(sp, spread[1], k, u)
                    sp.dma_start(table[:, u].rearrange("p a w -> p (a w)"),
                                 row(scr["dst_parts"], j).rearrange("o p w -> p (o w)")).then_inc(table_in[u], 16)
                    freed(sp, feat_done[1], k, u)
                    sp.dma_start(feat[3:FR, u, :], scr["edge_parts"][:, bass.ds(t, 1), :].rearrange("f o e -> f (o e)")).then_inc(feat_in[u], 16)

                def store(i, k, u):
                    ready(sp, rows_in, k, u, 16 * TG)
                    sp.dma_start(row(scr["rows_kept"], i).rearrange("o p w -> p (o w)"),
                                 rows[:, u].rearrange("p t w -> p (t w)")).then_inc(rows_kept[u], 16)

                staggered(sp, S, R, 2, load, store)
                for u in range(R):
                    sp.wait_ge(rows_kept[u], 16 * (S // R))

            @block.gpsimd
            def _(pool):
                def gather(i, k, u):
                    ready(pool, idx_made, k, u)
                    freed(pool, rows_kept, k, u, 16)
                    freed(pool, tmp_made[1], k, u)
                    pool.sem_inc(passed, 1)
                    for t in range(TG):
                        pool.indirect_dma_start(out=rows[:, u, t, :], out_offset=None, in_=scr["src_table"],
                                                in_offset=bass.IndirectOffsetOnAxis(ap=idx[:, u, t:t + 1], axis=0)).then_inc(rows_in[u], 16)

                staggered(pool, S, R, 0, none, gather)

            @block.tensor
            def _(pe):
                pe.wait_ge(w_laid, 16 * (3 + len(PRODUCTS)))
                pe.wait_ge(ones_set, 1)

                def body(i, k, u):
                    for hf in range(2):
                        if hf == 0:
                            ready(pe, feat_in, k, u, 16)
                        before(pe, enc_made[hf], k, u)
                        for t in range(HT):
                            e = (hf * HT + t) * P
                            last = nc.tensor.matmul(ps_f[hf][:, t, :], feat[:, u, e:e + P], w_rows[:], start=True, stop=True)
                        last.then_inc(feat_done[hf][u], 1)
                        if hf == 0:
                            ready(pe, hot_made, k, u)
                            ready(pe, table_in, k, u, 16)
                        before(pe, tmp_made[hf], k, u)
                        for t in range(HT):
                            e = (hf * HT + t) * P
                            for part in range(3):
                                last = nc.tensor.matmul(ps_d[hf][:, t, 0:DST_W], hot[:, u, e:e + P], table[:, u, part, :],
                                                        start=(part == 0), stop=(part == 2))
                        last.then_inc(spread[hf][u], 1)

                staggered(pe, S, R, 0, none, body)

            @block.scalar
            def _(act):
                def index(i, k, u):
                    freed(act, rows_in, k, u, 16 * TG)
                    nc.scalar.copy(idx[:, u, :], keep["idx_e"][:, bass.ds(i, 1), :].rearrange("p o t -> p (o t)")).then_inc(idx_made[u], 1)

                def encode(i, k, u):
                    for hf in range(2):
                        ready(act, feat_done[hf], k, u)
                        before(act, multiplied[hf], k, u)
                        nc.scalar.activation(enc[:, hf], ps_f[hf][:], ACT.Relu).then_inc(enc_made[hf][u], 1)

                staggered(act, S, R, 2, index, encode)

            @block.vector
            def _(dve):
                nc.vector.memset(feat[0:3], 1.0).then_inc(ones_set, 1)
                dve.wait_ge(w_in, 16)
                for part in range(3):
                    w = w_rest if part else w_edge
                    nc.vector.tensor_copy(w_parts[:, part, :], w[:]).then_inc(w_split, 1)
                    dve.wait_ge(w_split, part + 1)
                    if part < 2:
                        nc.vector.tensor_tensor(w_rest[:], w[:], w_parts[:, part, :], ALU.subtract).then_inc(w_left, 1)
                        dve.wait_ge(w_left, part + 1)

                def spreader(i, k, u):
                    ready(dve, rel_in, k, u, 16)
                    freed(dve, spread[1], k, u)
                    nc.vector.tensor_scalar(hot[:, u, :], relb[:, u, :], keep["iota_p"][:, 0:1], None, ALU.is_equal).then_inc(hot_made[u], 1)

                def body(i, k, u):
                    for hf in range(2):
                        ready(dve, enc_made[hf], k, u)
                        ready(dve, spread[hf], k, u)
                        before(dve, reduced[hf], k, u)
                        nc.vector.tensor_tensor(prod[:, hf], enc[:, hf], ps_d[hf][:, :, 0:C], ALU.mult).then_inc(multiplied[hf][u], 1)
                        if hf == 0:
                            ready(dve, rows_in, k, u, 16 * TG)
                        before(dve, scored[hf], k, u)
                        nc.vector.tensor_tensor(tmp[:, hf], ps_d[hf][:, :, C:DST_W], rows[:, u, hf * HT:(hf + 1) * HT, 0:H],
                                                ALU.add).then_inc(tmp_made[hf][u], 1)
                        ready(dve, multiplied[hf], k, u)
                        nc.vector.reduce_sum(red[:, hf].rearrange("p t h -> p (t h)"),
                                             prod[:, hf].rearrange("p t (h d) -> p (t h) d", d=HD), AX).then_inc(reduced[hf][u], 1)
                        ready(dve, tmp_made[hf], k, u)
                        ready(dve, reduced[hf], k, u)
                        nc.vector.tensor_tensor(keep["edge_a"][:, bass.ds(i, 1), hf * HT * H:(hf + 1) * HT * H],
                                                red[:, hf].rearrange("p t h -> p (t h)").unsqueeze(1),
                                                tmp[:, hf].rearrange("p t h -> p (t h)").unsqueeze(1), ALU.add).then_inc(scored[hf][u], 1)

                staggered(dve, S, R, 1, spreader, body)
        s.free()


def stage_softmax(nc, dims, ins, keep, scr):
    S = dims["S"]
    Q = S // 4
    CH = P // H
    L = S * GE // CH
    a = keep["edge_a"][:].rearrange("p s c -> p (s c)")
    PIECE = 4
    with ExitStack() as st:
        s = Kit(nc, st, "x_")
        b = keep["sums"][:, 0:L]
        pen_t = s.sb("pen", [P, L + 1], BF16)
        pen = pen_t[:]
        mid = s.sb("mid", [P, 1])
        ends = s.sb("ends", [P, 2])
        chain = s.sb("chain", [H, 2, CH])
        scanned = s.sb("scanned", [H, CH])
        carry8 = s.sb("carry8", [H, CH])
        carry = s.sb("carry", [P, 1])
        ps_x = [s.ps(f"ps_x{u}", [P, 4, P]) for u in range(2)]
        pen_in = s.sem("pen_in")
        slot = s.sb("slot", [P, 2, 4 * P])
        staged = s.sem2("staged")
        staged_b = s.sem2("staged_b")
        turned_ = s.sem2("turned")
        put = s.sem2("put")
        tail_turned = s.sem("tail_turned")
        tail_put = s.sem("tail_put")
        scores_out = s.sem("scores_out")
        scores_in = s.sem("scores_in")
        step = s.sem("step")
        ends_made = s.sem("ends_made")
        ends_out = s.sem("ends_out")
        ends_in = s.sem("ends_in")
        carry_made = s.sem("carry_made")
        carry_out = s.sem("carry_out")
        carry_in = s.sem("carry_in")
        shifted = s.sem("shifted")
        exps = s.sem("exps")
        exps_out = s.sem("exps_out")
        exps_in = s.sem("exps_in")
        turned_b = s.sem2("turned_b")
        put_b = s.sem2("put_b")
        tail_turned_b = s.sem("tail_turned_b")
        tail_put_b = s.sem("tail_put_b")
        G4 = Q // 4
        REST = Q % 4
        assert G4 % 2 == 0

        def stage_in(dve, src, staged, turned):
            def body(i, k, u):
                freed(dve, turned, k, u)
                nc.vector.tensor_copy(slot[:, u, :], src[:, bass.ds(i * 4 * P, 4 * P)]).then_inc(staged[u], 1)
            pairs(dve, G4, body)
            if REST:
                dve.wait_ge(turned[0], G4 // 2)
                nc.vector.tensor_copy(slot[:, 0, 0:REST * P], src[:, 4 * G4 * P:Q * P]).then_inc(staged[0], 1)

        def turn(pe, staged, turned, put_, t_turned):
            def body(i, k, u):
                ready(pe, staged, k, u)
                freed(pe, put_, k, u)
                for m in range(4):
                    last = nc.tensor.transpose(ps_x[u][:, m, :], slot[:, u, m * P:(m + 1) * P], keep["ident"][:])
                last.then_inc(turned[u], 1)
            pairs(pe, G4, body)
            if REST:
                pe.wait_ge(staged[0], G4 // 2 + 1)
                pe.wait_ge(put_[0], G4 // 2)
                for m in range(REST):
                    last = nc.tensor.transpose(ps_x[0][:, m, :], slot[:, 0, m * P:(m + 1) * P], keep["ident"][:])
                last.then_inc(t_turned, 1)

        def put_all(act, dst, turned, put_, t_turned, t_put):
            def body(i, k, u):
                ready(act, turned, k, u)
                nc.scalar.copy(dst[:, bass.ds(i * 512, 512)], ps_x[u][:].rearrange("p m e -> p (m e)")).then_inc(put_[u], 1)
            pairs(act, G4, body)
            if REST:
                act.wait_ge(t_turned, 1)
                nc.scalar.copy(dst[:, 4 * G4 * P:Q * P], ps_x[0][:, 0:REST, :].rearrange("p m e -> p (m e)")).then_inc(t_put, 1)

        def backwards(t, n, lo=0):
            v = t[:, lo:lo + n]
            return bass.AP(v.tensor, v.offset + n - 1, [v.ap[0], [-1, n]])

        by_step = lambda d: d.rearrange("h (q s t e) -> s t h q e", s=4, t=TG, e=P)
        by_chunk = lambda d: d.rearrange("h (c l) -> c h l", c=CH)

        with nc.Block() as block:
            @block.tensor
            def _(pe):
                turn(pe, staged, turned_, put, tail_turned)
                turn(pe, staged_b, turned_b, put_b, tail_turned_b)

            @block.sync
            def _(sp):
                for c in range(CH):
                    v = scr["pen_rows"].rearrange("s e -> (s e)")[c * L:(c + 1) * L + 1]
                    sp.dma_start(pen[c * H:(c + 1) * H, :], v.partition_broadcast(H)).then_inc(pen_in, 16)
                for u in range(2):
                    sp.wait_ge(put[u], G4 // 2)
                if REST:
                    sp.wait_ge(tail_put, 1)
                for m in range(CH):
                    sp.dma_start(by_step(scr["score_t"])[m // TG, m % TG],
                                 b[m * H:(m + 1) * H, :].rearrange("p (q e) -> p q e", e=P)).then_inc(scores_out, 16)
                sp.wait_ge(scores_out, 16 * CH)
                for c in range(CH):
                    sp.dma_start(a[c * H:(c + 1) * H, :], by_chunk(scr["score_t"])[c]).then_inc(scores_in, 16)
                for n in range(2):
                    sp.wait_ge(ends_made, n + 1)
                    sp.dma_start(scr["ends"], ends[:]).then_inc(ends_out, 16)
                    sp.wait_ge(ends_out, 16 * (n + 1))
                    for w in range(2):
                        sp.dma_start(chain[:, w, :], scr["ends"].rearrange("(c h) w -> w h c", h=H)[w],
                                     allow_slow_non_contiguous=True).then_inc(ends_in, 16)
                    sp.wait_ge(carry_made, n + 1)
                    sp.dma_start(scr["carry"], carry8[:]).then_inc(carry_out, 16)
                    sp.wait_ge(carry_out, 16 * (n + 1))
                    for c in range(CH):
                        sp.dma_start(carry[c * H:(c + 1) * H, :], scr["carry"][:, c:c + 1],
                                     allow_slow_non_contiguous=True).then_inc(carry_in, 16)
                sp.wait_ge(exps, PIECE)
                for c in range(CH):
                    sp.dma_start(by_chunk(scr["exp_t"])[c], a[c * H:(c + 1) * H, :]).then_inc(exps_out, 16)
                sp.wait_ge(exps_out, 16 * CH)
                for m in range(CH):
                    sp.dma_start(b[m * H:(m + 1) * H, :].rearrange("p (q e) -> p q e", e=P),
                                 by_step(scr["exp_t"])[m // TG, m % TG]).then_inc(exps_in, 16)

            @block.scalar
            def _(act):
                put_all(act, b, turned_, put, tail_turned, tail_put)
                for m in range(PIECE):
                    act.wait_ge(shifted, m + 1)
                    cut = slice(m * L // PIECE, (m + 1) * L // PIECE)
                    nc.scalar.activation(a[:, cut], a[:, cut], ACT.Exp).then_inc(exps, 1)
                put_all(act, a, turned_b, put_b, tail_turned_b, tail_put_b)

            @block.vector
            def _(dve):
                n = [0]

                def link(ins_):
                    n[0] += 1
                    ins_.then_inc(step, 1)
                    dve.wait_ge(step, n[0])

                stage_in(dve, a, staged, turned_)
                dve.wait_ge(pen_in, 16 * CH)
                link(nc.vector.tensor_reduce(mid[:], pen[:, 1:L], AX, ALU.min))
                dve.wait_ge(scores_in, 16 * CH)
                link(nc.vector.scalar_tensor_tensor(out=a, in0=a, scalar=SLOPE, in1=a, op0=ALU.mult, op1=ALU.max))

                def chunks(n_, edge_cut, value):
                    link(nc.vector.tensor_tensor(ends[:, 1:2], mid[:], edge_cut, ALU.min))
                    nc.vector.tensor_copy(ends[:, 0:1], value).then_inc(ends_made, 1)
                    dve.wait_ge(ends_in, 32 * (n_ + 1))
                    rev = n_ == 1
                    va, cu, out = chain[:, 0, :], chain[:, 1, :], scanned[:]
                    if rev:
                        va, cu, out = backwards(va, CH), backwards(cu, CH), backwards(out, CH)
                    link(nc.vector.tensor_tensor_scan(out, cu, va, NEG, ALU.add, ALU.max))
                    if rev:
                        link(nc.vector.memset(carry8[:, CH - 1:CH], NEG))
                        nc.vector.tensor_copy(carry8[:, 0:CH - 1], scanned[:, 1:CH]).then_inc(carry_made, 1)
                    else:
                        link(nc.vector.memset(carry8[:, 0:1], NEG))
                        nc.vector.tensor_copy(carry8[:, 1:CH], scanned[:, 0:CH - 1]).then_inc(carry_made, 1)
                    dve.wait_ge(carry_in, 16 * CH * (n_ + 1))

                link(nc.vector.tensor_tensor_scan(b, pen[:, 0:L], a, NEG, ALU.add, ALU.max))
                chunks(0, pen[:, 0:1], b[:, L - 1:L])
                link(nc.vector.tensor_tensor_scan(b, pen[:, 0:L], a, carry[:, 0:1], ALU.add, ALU.max))
                cut_b, b_rev = backwards(pen, L, 1), backwards(b, L)
                link(nc.vector.tensor_tensor_scan(b_rev, cut_b, b_rev, NEG, ALU.add, ALU.max))
                chunks(1, pen[:, L:L + 1], b[:, 0:1])
                link(nc.vector.tensor_tensor_scan(b_rev, cut_b, b_rev, carry[:, 0:1], ALU.add, ALU.max))
                for m in range(PIECE):
                    cut = slice(m * L // PIECE, (m + 1) * L // PIECE)
                    nc.vector.tensor_tensor(a[:, cut], a[:, cut], b[:, cut], ALU.subtract).then_inc(shifted, 1)
                dve.wait_ge(exps_in, 16 * CH)
                if REST:
                    dve.wait_ge(tail_turned, 1)
                stage_in(dve, b, staged_b, turned_b)
        s.free()


def stage_aggregate(nc, dims, ins, keep, scr):
    S, NT = dims["S"], dims["NT"]
    R = 4
    sums = keep["sums"][:, 0:NT * SRC_W].rearrange("p (j w) -> p j w", w=SRC_W)
    with ExitStack() as st:
        s = Kit(nc, st, "g_")
        rows = s.sb("rows", [P, R, TG, SRC_W])
        hot = s.sb("hot", [P, R, TG, P])
        ps_a = [s.ps(f"ps_a{u}", [P, SRC_W]) for u in range(R)]
        rows_in = s.sem2("rows_in", R)
        hot_made = s.sem2("hot_made", R)
        weighted = s.sem2("weighted", R)
        weighted_b = s.sem2("weighted_b", R)
        exps_put = s.sem2("exps_put", R)
        summed = s.sem2("summed", R)
        added = s.sem2("added", R)
        cleared = s.sem("cleared")

        HT = TG // 2

        def weights(i, u, lo, hi):
            exps = keep["edge_a"][:, bass.ds(i, 1), lo * H:hi * H].rearrange("p o (t h) -> p (o t) h", h=H)
            return (rows[:, u, lo:hi, H:SRC_W].rearrange("p t (h d) -> p t h d", d=HD),
                    exps.unsqueeze(3).to_broadcast([P, hi - lo, H, HD]))

        with nc.Block() as block:
            @block.sync
            def _(sp):
                def load(i, k, u):
                    freed(sp, summed, k, u)
                    sp.dma_start(rows[:, u].rearrange("p t w -> p (t w)"),
                                 row(scr["rows_kept"], i).rearrange("o p w -> p (o w)")).then_inc(rows_in[u], 16)

                staggered(sp, S, R, 0, none, load)

            @block.scalar
            def _(act):
                def put_exps(i, k, u):
                    ready(act, rows_in, k, u, 16)
                    nc.scalar.copy(rows[:, u, :, 0:H], keep["edge_a"][:, bass.ds(i, 1), :].rearrange("p o (t h) -> p (o t) h", t=TG)).then_inc(exps_put[u], 1)

                staggered(act, S, R, 0, none, put_exps)

            @block.gpsimd
            def _(pool):
                def weigh(i, k, u):
                    ready(pool, rows_in, k, u, 16)
                    v, exps = weights(i, u, HT, TG)
                    nc.gpsimd.tensor_tensor(v, v, exps, ALU.mult).then_inc(weighted_b[u], 1)

                staggered(pool, S, R, 0, none, weigh)

            @block.tensor
            def _(pe):
                def body(i, k, u):
                    ready(pe, hot_made, k, u)
                    ready(pe, weighted, k, u)
                    ready(pe, weighted_b, k, u)
                    ready(pe, exps_put, k, u)
                    freed(pe, added, k, u)
                    for t in range(TG):
                        last = nc.tensor.matmul(ps_a[u][:], hot[:, u, t, :], rows[:, u, t, :], start=(t == 0), stop=(t == TG - 1))
                    last.then_inc(summed[u], 1)

                staggered(pe, S, R, 0, none, body)

            @block.vector
            def _(dve):
                nc.vector.memset(sums, 0.0).then_inc(cleared, 1)
                dve.wait_ge(cleared, 1)

                def weigh(i, k, u):
                    freed(dve, summed, k, u)
                    nc.vector.tensor_tensor(hot[:, u], keep["rel_e"][:, bass.ds(i, 1), :].rearrange("p o t -> p (o t)").unsqueeze(2).to_broadcast([P, TG, P]),
                                            keep["iota_row"][:].unsqueeze(1).to_broadcast([P, TG, P]), ALU.is_equal).then_inc(hot_made[u], 1)
                    ready(dve, rows_in, k, u, 16)
                    v, exps = weights(i, u, 0, HT)
                    nc.vector.tensor_tensor(v, v, exps, ALU.mult).then_inc(weighted[u], 1)

                def add(i, k, u):
                    j = dve.value_load(keep["j_of"][0:1, bass.ds(i, 1)], min_val=0, max_val=NT - 1)
                    ready(dve, summed, k, u)
                    before(dve, added, k, u)
                    y = sums[:, bass.ds(j, 1), :].rearrange("p o w -> p (o w)")
                    nc.vector.tensor_tensor(y, ps_a[u][:], y, ALU.add).then_inc(added[u], 1)

                staggered(dve, S, R, 2, weigh, add)
        s.free()


def stage_combine(nc, dims, ins, keep, scr):
    NT = dims["NT"]
    SB = 7
    NG = NT // SB
    BB = P // EXPERTS
    NB = -(-NT // BB)
    V = nc.vector
    sums = keep["sums"][:, 0:NT * SRC_W].rearrange("p (j w) -> p j w", w=SRC_W)
    x1, gate = keep["y_all"], keep["gate"]
    with ExitStack() as st:
        s = Kit(nc, st, "b_")
        wr = s.sb("wr", [P, 2, EXPERTS])
        br = s.sb("br", [P, EXPERTS])
        bo = s.sb("bo", [P, BB, C])
        xm = s.sb("xm", [P, 2, SB, C])
        den = s.sb("den", [P, NT, H])
        stats = s.sb("stats", [P, NT, 6])
        t0 = s.sb("t0", [P, NT])
        t1 = s.sb("t1", [P, NT])
        mean = s.sb("mean", [P, NT])
        rstd = s.sb("rstd", [P, NT])
        nmr = s.sb("nmr", [P, NT])
        xn = s.sb("xn", [P, 2, C])
        xT = s.sb("xT", [P, 2, 2, P])
        lg = s.sb("lg", [P, NT, EXPERTS])
        gateT = s.sb("gateT", [P, NB, P])
        ps_t = [s.ps(f"ps_t{u}", [P, 2, P]) for u in range(2)]
        ps_l = [s.ps(f"ps_l{u}", [P, EXPERTS]) for u in range(2)]
        ps_g = s.ps("ps_g", [P, NB, P])
        ps_b = [s.ps(f"ps_b{u}", [P, 2, C]) for u in range(2)]
        w_in = s.sem("w_in")
        xm_in = s.sem2("xm_in")
        x1_made = s.sem2("x1_made")
        step = s.sem("step")
        stats_made = s.sem("stats_made")
        var_made = s.sem("var_made")
        std_made = s.sem("std_made")
        norm_made = s.sem("norm_made")
        xn_made = s.sem2("xn_made")
        turned_x = s.sem2("turned_x")
        xT_made = s.sem2("xT_made")
        xT_kept = s.sem2("xT_kept")
        logits_done = s.sem2("logits_done")
        lg_made = s.sem2("lg_made")
        shifted = s.sem("shifted")
        exps = s.sem("exps")
        gate_made = s.sem("gate_made")
        gate_turned = s.sem("gate_turned")
        gateT_made = s.sem("gateT_made")
        bias_done = s.sem2("bias_done")
        bias_added = s.sem2("bias_added")
        NP = -(-NT // 2)

        with nc.Block() as block:
            @block.sync
            def _(sp):
                sp.dma_start(wr[:], ins["Wr"]).then_inc(w_in, 16)
                sp.dma_start(br[:], ins["br"].partition_broadcast(P)).then_inc(w_in, 16)
                sp.dma_start(bo[:], ins["bo_blocks"]).then_inc(w_in, 16)

                def load(i, k, u):
                    freed(sp, x1_made, k, u)
                    sp.dma_start(xm[:, u], scr["x_mix"][bass.ds(i * SB, SB)].rearrange("g p w -> p g w")).then_inc(xm_in[u], 16)

                pairs(sp, NG, load)

            @block.vector
            def _(dve):
                n = [0]

                def link(ins_):
                    n[0] += 1
                    ins_.then_inc(step, 1)
                    dve.wait_ge(step, n[0])

                link(V.tensor_scalar(den[:], sums[:, :, 0:H], DEN_MIN, None, ALU.max))
                link(V.reciprocal(den[:], den[:]))
                link(V.tensor_tensor(x1.rearrange("p j (h d) -> p j h d", h=H), x1.rearrange("p j (h d) -> p j h d", h=H),
                                     den[:].unsqueeze(3).to_broadcast([P, NT, H, HD]), ALU.mult))

                def residual(i, k, u):
                    ready(dve, xm_in, k, u, 16)
                    v = x1[:, bass.ds(i * SB, SB), :]
                    V.tensor_tensor(v, v, xm[:, u], ALU.add).then_inc(x1_made[u], 1)

                for g in range(NG + 1):
                    if g < NG:
                        residual(g, g // 2, g % 2)
                    if g > 0:
                        ready(dve, x1_made, (g - 1) // 2, (g - 1) % 2)
                        for i in range((g - 1) * SB, g * SB):
                            V.bn_stats(stats[:, i, :], x1[:, i, :]).then_inc(stats_made, 1)
                dve.wait_ge(stats_made, NT)
                link(V.tensor_tensor(t0[:], stats[:, :, 1], stats[:, :, 4], ALU.add))
                link(V.tensor_scalar(mean[:], t0[:], 0.5, None, ALU.mult))
                link(V.tensor_tensor(t0[:], stats[:, :, 1], stats[:, :, 4], ALU.subtract))
                link(V.tensor_tensor(t0[:], t0[:], t0[:], ALU.mult))
                link(V.tensor_scalar(t0[:], t0[:], 0.25, LN_EPS, ALU.mult, ALU.add))
                link(V.tensor_tensor(t1[:], stats[:, :, 2], stats[:, :, 5], ALU.add))
                V.scalar_tensor_tensor(out=t1[:], in0=t1[:], scalar=1.0 / C, in1=t0[:], op0=ALU.mult, op1=ALU.add).then_inc(var_made, 1)
                dve.wait_ge(std_made, 1)
                link(V.reciprocal(rstd[:], t1[:]))
                V.scalar_tensor_tensor(out=nmr[:], in0=mean[:], scalar=-1.0, in1=rstd[:], op0=ALU.mult, op1=ALU.mult).then_inc(norm_made, 1)
                dve.wait_ge(w_in, 48)

                def keep_turned(i, k, u):
                    ready(dve, xT_made, k, u)
                    V.tensor_copy(keep["xT"][:, :, bass.ds(i * P, P)], xT[:, u]).then_inc(xT_kept[u], 1)

                def logits(i, k, u):
                    ready(dve, logits_done, k, u)
                    V.tensor_tensor(lg[:, bass.ds(i, 1), :], ps_l[u][:].unsqueeze(1), br[:].unsqueeze(1), ALU.add).then_inc(lg_made[u], 1)

                skewed(dve, NT, keep_turned, logits)
                ready(dve, lg_made, NT // 2, 0)
                link(V.reduce_max(t0[:], lg[:], AX))
                V.tensor_tensor(lg[:], lg[:], t0[:].unsqueeze(2).to_broadcast([P, NT, EXPERTS]), ALU.subtract).then_inc(shifted, 1)
                dve.wait_ge(exps, 1)
                link(V.reduce_sum(t0[:], lg[:], AX))
                link(V.reciprocal(t0[:], t0[:]))
                V.tensor_tensor(gate[:], lg[:], t0[:].unsqueeze(2).to_broadcast([P, NT, EXPERTS]), ALU.mult).then_inc(gate_made, 1)
                for n_ in range(NP):
                    k, u = n_ // 2, n_ % 2
                    b = min(2, NT - 2 * n_)
                    ready(dve, bias_done, k, u)
                    v = x1[:, 2 * n_:2 * n_ + b, :]
                    V.tensor_tensor(v, ps_b[u][:, 0:b, :], v, ALU.add).then_inc(bias_added[u], 1)

            @block.scalar
            def _(act):
                act.wait_ge(var_made, 1)
                nc.scalar.activation(t1[:], t1[:], ACT.Sqrt).then_inc(std_made, 1)
                act.wait_ge(norm_made, 1)

                def normalise(i, k, u):
                    freed(act, turned_x, k, u)
                    nc.scalar.activation(xn[:, u, :], x1[:, bass.ds(i, 1), :].rearrange("p o c -> p (o c)"), ACT.Identity,
                                         scale=rstd[:, bass.ds(i, 1)], bias=nmr[:, bass.ds(i, 1)]).then_inc(xn_made[u], 1)

                def put(i, k, u):
                    ready(act, turned_x, k, u)
                    freed(act, logits_done, k, u)
                    freed(act, xT_kept, k, u)
                    nc.scalar.copy(xT[:, u], ps_t[u][:]).then_inc(xT_made[u], 1)

                skewed(act, NT, normalise, put)
                act.wait_ge(shifted, 1)
                nc.scalar.activation(lg[:], lg[:], ACT.Exp).then_inc(exps, 1)
                act.wait_ge(gate_turned, 1)
                for b in range(NB):
                    m = min(P, NT * EXPERTS - b * P)
                    nc.scalar.copy(gateT[0:m, b, :], ps_g[0:m, b, :]).then_inc(gateT_made, 1)

            @block.tensor
            def _(pe):
                pe.wait_ge(w_in, 48)

                def turn(i, k, u):
                    ready(pe, xn_made, k, u)
                    freed(pe, xT_made, k, u)
                    for c in range(2):
                        last = nc.tensor.transpose(ps_t[u][:, c, :], xn[:, u, c * P:(c + 1) * P], keep["ident"][:])
                    last.then_inc(turned_x[u], 1)

                def logits(i, k, u):
                    ready(pe, xT_made, k, u)
                    freed(pe, lg_made, k, u)
                    for c in range(2):
                        last = nc.tensor.matmul(ps_l[u][:], xT[:, u, c, :], wr[:, c, :], start=(c == 0), stop=(c == 1))
                    last.then_inc(logits_done[u], 1)

                skewed(pe, NT, turn, logits)
                pe.wait_ge(gate_made, 1)
                flat = gate[:].rearrange("p j e -> p (j e)")
                for b in range(NB):
                    m = min(P, NT * EXPERTS - b * P)
                    last = nc.tensor.transpose(ps_g[0:m, b, :], flat[:, b * P:b * P + m], keep["ident"][:])
                last.then_inc(gate_turned, 1)
                pe.wait_ge(gateT_made, NB)
                for n in range(NP):
                    k, u = n // 2, n % 2
                    freed(pe, bias_added, k, u)
                    for i in range(2 * n, min(NT, 2 * n + 2)):
                        m = min(P, NT * EXPERTS - i // BB * P)
                        last = nc.tensor.matmul(ps_b[u][:, i % 2, :], gateT[0:m, i // BB, :], bo[0:m, i % BB, :], start=True, stop=True)
                    last.then_inc(bias_done[u], 1)
        s.free()


def stage_experts(nc, dims, ins, keep, scr, out):
    NT = dims["NT"]
    SB = 7
    NS = NT // SB
    W = SB * P // 2
    with ExitStack() as st:
        s = Kit(nc, st, "e_")
        w = {n: s.sb(n, [P, EXPERTS, 2, C]) for n in ("W1", "W2", "Wo")}
        norm = {n: s.sb(n, [P, EXPERTS, 2]) for n in ("b1", "g1", "be1", "m1", "v1", "b2", "g2", "be2", "m2", "v2")}
        scale = {n: s.sb(f"scale{n}", [P, EXPERTS, 2]) for n in "12"}
        shift = {n: s.sb(f"shift{n}", [P, EXPERTS, 2]) for n in "12"}
        h1 = s.sb("h1", [P, 2, 2 * W])
        h2 = s.sb("h2", [P, 2, 2 * W])
        ps = [s.ps(f"ps{b}", [P, 512]) for b in range(4)]
        ps_o = [s.ps(f"ps_o{b}", [P, 2, C]) for b in range(4)]
        norm_in = s.sem("norm_in")
        w_in = [s.sem(f"w_in{e}") for e in range(EXPERTS)]
        step = s.sem("step")
        veps_made = s.sem("veps_made")
        std_made = s.sem("std_made")
        norm_made = s.sem("norm_made")
        l1_done = [s.sem(f"l1_done{q}") for q in range(4)]
        h1_made = [s.sem(f"h1_made{q}") for q in range(4)]
        l2_done = [s.sem(f"l2_done{q}") for q in range(4)]
        h2_made = [s.sem(f"h2_made{q}") for q in range(4)]
        o_done = [s.sem(f"o_done{b}") for b in range(4)]
        o_added = [s.sem(f"o_added{b}") for b in range(4)]
        out_stored = s.sem("out_stored")

        with nc.Block() as block:
            @block.sync
            def _(sp):
                for n in norm:
                    sp.dma_start(norm[n][:], ins[n]).then_inc(norm_in, 16)
                for e in range(EXPERTS):
                    for n in w:
                        sp.dma_start(w[n][:, e], ins[n][:, e]).then_inc(w_in[e], 16)
                def body(i):
                    sp.wait_ge(o_added[3], EXPERTS * (i + 1))
                    sp.dma_start(out[:, bass.ds(i * SB, SB), :], keep["y_all"][:, bass.ds(i * SB, SB), :]).then_inc(out_stored, 16)

                turns(sp, NS, body)
                sp.wait_ge(out_stored, 16 * NS)

            @block.vector
            def _(dve):
                n = [0]

                def link(ins_):
                    n[0] += 1
                    ins_.then_inc(step, 1)
                    dve.wait_ge(step, n[0])

                dve.wait_ge(norm_in, 160)
                V = nc.vector
                for q in "12":
                    V.tensor_scalar(norm["v" + q][:], norm["v" + q][:], BN_EPS, None, ALU.add).then_inc(veps_made, 1)
                for m, q in enumerate("12"):
                    dve.wait_ge(std_made, m + 1)
                    link(V.reciprocal(norm["v" + q][:], norm["v" + q][:]))
                    link(V.tensor_tensor(scale[q][:], norm["g" + q][:], norm["v" + q][:], ALU.mult))
                    link(V.tensor_tensor(shift[q][:], norm["b" + q][:], norm["m" + q][:], ALU.subtract))
                    link(V.tensor_tensor(shift[q][:], shift[q][:], scale[q][:], ALU.mult))
                    V.tensor_tensor(shift[q][:], shift[q][:], norm["be" + q][:], ALU.add).then_inc(norm_made, 1)
                def body(i):
                    for e in range(EXPERTS):
                        turn = i * EXPERTS + e
                        for b in range(SB):
                            q, r = b // 2, b % 2
                            if r == 0:
                                dve.wait_ge(o_done[q], turn + 1)
                            pq = 2 if q < 3 else 1
                            wait(dve, o_added[q], turn * pq)
                            y = keep["y_all"][:, bass.ds(i * SB + b, 1), :].rearrange("p o c -> p (o c)")
                            V.scalar_tensor_tensor(out=y, in0=ps_o[q][:, r, :], scalar=keep["gate"][:, bass.ds(i * SB + b, 1), e:e + 1].rearrange("p o e -> p (o e)"),
                                                   in1=y, op0=ALU.mult, op1=ALU.add).then_inc(o_added[q], 1)

                turns(dve, NS, body)

            @block.scalar
            def _(act):
                for m, q in enumerate("12"):
                    act.wait_ge(veps_made, m + 1)
                    nc.scalar.activation(norm["v" + q][:], norm["v" + q][:], ACT.Sqrt).then_inc(std_made, 1)
                act.wait_ge(norm_made, 2)

                def body(i):
                    for e in range(EXPERTS):
                        turn = i * EXPERTS + e
                        for q in range(4):
                            m, hf = q // 2, q % 2
                            act.wait_ge(l1_done[q], turn + 1)
                            wait(act, l2_done[3], turn)
                            nc.scalar.activation(h1[:, m, hf * W:(hf + 1) * W], ps[q][:, 0:W], ACT.Relu,
                                                 scale=scale["1"][:, e, m:m + 1], bias=shift["1"][:, e, m:m + 1]).then_inc(h1_made[q], 1)
                        for q in range(4):
                            m, hf = q // 2, q % 2
                            act.wait_ge(l2_done[q], turn + 1)
                            wait(act, o_done[3], turn)
                            nc.scalar.activation(h2[:, m, hf * W:(hf + 1) * W], ps[q][:, 0:W], ACT.Relu,
                                                 scale=scale["2"][:, e, m:m + 1], bias=shift["2"][:, e, m:m + 1]).then_inc(h2_made[q], 1)

                turns(act, NS, body)

            @block.tensor
            def _(pe):
                def body(i):
                    for e in range(EXPERTS):
                        turn = i * EXPERTS + e
                        pe.wait_ge(w_in[e], 48)
                        for q in range(4):
                            m, hf = q // 2, q % 2
                            wait(pe, h2_made[q], turn)
                            for c in range(2):
                                last = nc.tensor.matmul(ps[q][:, 0:W], w["W1"][:, e, c, m * P:(m + 1) * P],
                                                        keep["xT"][:, c, bass.ds(i * 2 * W + hf * W, W)],
                                                        start=(c == 0), stop=(c == 1))
                            last.then_inc(l1_done[q], 1)
                        for q in range(4):
                            m, hf = q // 2, q % 2
                            pe.wait_ge(h1_made[hf], turn + 1)
                            pe.wait_ge(h1_made[2 + hf], turn + 1)
                            pe.wait_ge(h1_made[q], turn + 1)
                            for c in range(2):
                                last = nc.tensor.matmul(ps[q][:, 0:W], w["W2"][:, e, c, m * P:(m + 1) * P],
                                                        h1[:, c, hf * W:(hf + 1) * W], start=(c == 0), stop=(c == 1))
                            last.then_inc(l2_done[q], 1)
                        for b in range(SB):
                            q, r = b // 2, b % 2
                            if b in (0, SB // 2):
                                for m in range(2):
                                    pe.wait_ge(h2_made[2 * m + (b > 0)], turn + 1)
                            if r == 0:
                                wait(pe, o_added[q], turn * (2 if q < 3 else 1))
                            for c in range(2):
                                last = nc.tensor.matmul(ps_o[q][:, r, :], h2[:, c, b * P:(b + 1) * P], w["Wo"][:, e, c, :],
                                                        start=(c == 0), stop=(c == 1))
                            if r == 1 or b == SB - 1:
                                last.then_inc(o_done[q], 1)

                turns(pe, NS, body)
        s.free()


def build(nc, dims, ins, out):
    NT, S = dims["NT"], dims["S"]

    def dram(name, shape, dt=F32):
        return nc.dram_tensor("scratch_" + name, shape, dt, kind="Internal").ap()

    scr = dict(
        src_rows=dram("src_rows", (NT, P, SRC_W)), dst_parts=dram("dst_parts", (NT, P, 3 * DST_W), BF16),
        q_rows=dram("q_rows", (NT, P, H * EXT)), x_mix=dram("x_mix", (NT, P, C)),
        rel_rows=dram("rel_rows", (512, GE), BF16), pen_rows=dram("pen_rows", (512, GE), BF16),
        rows_kept=dram("rows_kept", (S, P, TG * SRC_W)), score_t=dram("score_t", (H, S * GE)),
        exp_t=dram("exp_t", (H, S * GE)), ends=dram("ends", (P, 2)), carry=dram("carry", (H, P // H)),
        edge_parts=dram("edge_parts", (EF * len(PRODUCTS), dims["T"], GE), BF16))
    scr["src_table"] = scr["src_rows"].rearrange("t p w -> (t p) w")

    with ExitStack() as whole:
        kit = Kit(nc, whole, "k_")
        keep = dict(ident=kit.sb("ident", [P, P]), iota_row=kit.sb("iota_row", [P, P]), iota_p=kit.sb("iota_p", [P, 1]))
        with ExitStack() as part:
            kit = Kit(nc, part, "kn_")
            keep.update(
                x_all=kit.sb("x_all", [P, NT, C]), w_h=kit.sb("w_h", [P, 2, ALL_W]), w_qkv=kit.sb("w_qkv", [P, 2, 3 * C]),
                b_qkv=kit.sb("b_qkv", [P, 3 * C]), w_proj=kit.sb("w_proj", [P, 2, C]), b_res=kit.sb("b_res", [P, 2, C]),
                c_out=kit.sb("c_out", [P, 2 * H]), c_in=kit.sb("c_in", [P, 2 * H]), in_range=kit.sb("in_range", [P, 1]),
                c_pair=kit.sb("c_pair", [P, 1]), rstd=kit.sb("rstd", [P, NT]), nmr=kit.sb("nmr", [P, NT]),
                g_sum=kit.sb("g_sum", [P, H * PB, VE]))
            stage_constants(nc, None, dims, ins, keep)
            stage_nodes(nc, None, dims, ins, keep, scr)
            stage_mix(nc, None, dims, ins, keep, scr)
        kit = Kit(nc, whole, "ky_")
        keep["sums"] = kit.sb("sums", [P, max(NT * SRC_W, S * GE * H // P)])
        with ExitStack() as part:
            kit = Kit(nc, part, "ke_")
            keep.update(
                t_of=kit.sb("t_of", [1, S], I32), j_of=kit.sb("j_of", [1, S], I32), 
                idx_e=kit.sb("idx_e", [P, 512, TG], I32), rel_e=kit.sb("rel_e", [P, 512, TG]))
            stage_plan(nc, dims, ins, keep, scr)
            keep["edge_a"] = kit.sb("edge_a", [P, S, TG * H])
            stage_scores(nc, dims, ins, keep, scr)
            stage_softmax(nc, dims, ins, keep, scr)
            stage_aggregate(nc, dims, ins, keep, scr)
        with ExitStack() as part:
            kit = Kit(nc, part, "kx_")
            keep.update(xT=kit.sb("xT", [P, 2, NT * P]), y_all=keep["sums"][:, 0:NT * SRC_W].rearrange("p (j w) -> p j w", w=SRC_W)[:, :, H:SRC_W],
                        gate=kit.sb("gate", [P, NT, EXPERTS]))
            stage_combine(nc, dims, ins, keep, scr)
            stage_experts(nc, dims, ins, keep, scr, out)


def kernel(**inputs):
    import numpy as np
    import concourse.bacc as bacc
    from concourse.bass_utils import run_bass_kernel_spmd

    arrays, dims = lay_out(inputs)
    nc = bacc.Bacc("TRN2", target_bir_lowering=False, num_devices=1)
    ins = {n: nc.dram_tensor("in_" + n, a.shape, mybir.dt.from_np(a.dtype), kind="ExternalInput").ap() for n, a in arrays.items()}
    out = nc.dram_tensor("out_rows", (dims["NT"] * P, C), F32, kind="ExternalOutput").ap()
    build(nc, dims, ins, out.rearrange("(t p) c -> p t c", p=P))
    r = run_bass_kernel_spmd(nc, [{"in_" + n: np.ascontiguousarray(a) for n, a in arrays.items()}], core_ids=[0])
    return r.results[0]["out_rows"][:dims["N"]]
```
